# Optimizing a Trainium2 kernel written in Bass

```python
import numpy as np
import jax
import jax.numpy as jnp

def _softmax(x, axis=-1):
    return jax.nn.softmax(x, axis=axis)

def _gelu(x):
    return jax.nn.gelu(x, approximate=True)

def _silu(x):
    return jax.nn.silu(x)

def _sigmoid(x):
    return jax.nn.sigmoid(x)

def _layernorm(x, axis=-1, eps=1e-05):
    m = jnp.mean(x, axis=axis, keepdims=True)
    v = jnp.var(x, axis=axis, keepdims=True)
    return (x - m) / jnp.sqrt(v + eps)

def _scatter_add(tgt, idx, src, axis=0):
    return tgt.at[idx].add(src)

def _segment_sum(src, seg, n):
    return jax.ops.segment_sum(src, seg, n)
kernel_name = 'mk_seq_postln_d1_jaxref_r4_360aa1'

def setup_inputs(seed: int=0):
    np.random.seed(seed)
    _w = jnp.asarray

    def _L0_attn_setup():
        import math
        import jax, jax.numpy as jnp
        import numpy as np
        EPS_SUM = 1e-07
        EPS_NORM = 1e-12

        def _l2norm(x, axis):
            n = jnp.sqrt(jnp.sum(x * x, axis=axis, keepdims=True))
            return x / jnp.maximum(n, EPS_NORM)
        key = jax.random.key(seed)
        ks = jax.random.split(key, 5)
        b, N, C = (4, 1024, 256)
        x = jax.random.normal(ks[0], (b, N, C), dtype=jnp.float32)
        Wqkv = jax.random.normal(ks[1], (C, 3 * C), dtype=jnp.float32) / math.sqrt(C)
        bqkv = jax.random.normal(ks[2], (3 * C,), dtype=jnp.float32) * 0.01
        Wln = jax.random.normal(ks[3], (C, C), dtype=jnp.float32) / math.sqrt(C)
        bln = jax.random.normal(ks[4], (C,), dtype=jnp.float32) * 0.01
        return {'x': x, 'Wqkv': Wqkv, 'bqkv': bqkv, 'Wln': Wln, 'bln': bln}
    _L0_attn_in = _L0_attn_setup()

    def _L0_ffn_setup():
        import jax, jax.numpy as jnp
        import numpy as np
        B, S, D = (4, 1024, 256)
        E, H = (16, 128)
        key = jax.random.key(seed)
        k0, k1, k2, k3 = jax.random.split(key, 4)
        std = 1.0 / np.sqrt(D)
        input_tensor = jax.random.normal(k0, (B, S, D), dtype=jnp.float32)
        expert_sel = jax.random.normal(k1, (E, D), dtype=jnp.float32) * std
        keys = jax.random.normal(k2, (E, D, H), dtype=jnp.float32) * std
        values = jax.random.normal(k3, (E, H, D), dtype=jnp.float32) * (1.0 / np.sqrt(E * H))
        return {'input_tensor': input_tensor, 'expert_sel': expert_sel, 'keys': keys, 'values': values}
    _L0_ffn_in = _L0_ffn_setup()
    _d = {'L0_attn_x': _L0_attn_in['x'], 'L0_attn_Wqkv': _L0_attn_in['Wqkv'], 'L0_attn_bqkv': _L0_attn_in['bqkv'], 'L0_attn_Wln': _L0_attn_in['Wln'], 'L0_attn_bln': _L0_attn_in['bln'], 'L0_ffn_expert_sel': _L0_ffn_in['expert_sel'], 'L0_ffn_keys': _L0_ffn_in['keys'], 'L0_ffn_values': _L0_ffn_in['values']}
    _x0 = _d['L0_attn_x']
    _d['L0_attn_x'] = jax.random.normal(jax.random.fold_in(jax.random.key(seed), 1), (8, 1024, 256), dtype=_x0.dtype)
    del _x0
    return _d

def reference(L0_attn_x, L0_attn_Wqkv, L0_attn_bqkv, L0_attn_Wln, L0_attn_bln, L0_ffn_expert_sel, L0_ffn_keys, L0_ffn_values):

    def _L0_attn_ref(x, Wqkv, bqkv, Wln, bln):
        import math
        import jax, jax.numpy as jnp
        import numpy as np
        EPS_SUM = 1e-07
        EPS_NORM = 1e-12

        def _l2norm(x, axis):
            n = jnp.sqrt(jnp.sum(x * x, axis=axis, keepdims=True))
            return x / jnp.maximum(n, EPS_NORM)
        b, N, C = x.shape
        qkv = x @ Wqkv + bqkv
        q, k, v = jnp.split(qkv, 3, axis=2)
        q = q - q.mean(axis=2, keepdims=True)
        k = k - k.mean(axis=2, keepdims=True)
        q2 = q * q
        k2 = k * k
        q2 = q2 / (q2.sum(axis=2, keepdims=True) + EPS_SUM)
        q2 = _l2norm(q2, axis=-1)
        k2 = k2 / (k2.sum(axis=2, keepdims=True) + EPS_SUM)
        k2 = _l2norm(k2, axis=-2)
        kv = jnp.einsum('bnc,bnd->bcd', k2, v)
        t2 = jnp.einsum('bnc,bcd->bnd', q2, kv) / math.sqrt(N)
        return (v + t2) @ Wln + bln

    def _L0_ffn_ref(input_tensor, expert_sel, keys, values):
        import jax, jax.numpy as jnp
        import numpy as np
        B, S, D = (4, 1024, 256)
        E, H = (16, 128)
        sel = jax.nn.sigmoid(jnp.einsum('bsd,ed->bse', input_tensor, expert_sel))
        scores = jax.nn.relu(jnp.einsum('bsd,edh->bseh', input_tensor, keys))
        out = jnp.einsum('bseh,ehv,bse->bsv', scores, values, sel)
        return out
    x = L0_attn_x
    x = _layernorm(x + _L0_attn_ref(x, L0_attn_Wqkv, L0_attn_bqkv, L0_attn_Wln, L0_attn_bln), axis=-1)
    x = _layernorm(x + _L0_ffn_ref(x, L0_ffn_expert_sel, L0_ffn_keys, L0_ffn_values), axis=-1)
    return x

_drawn_inputs = setup_inputs


def setup_inputs(seed=0):
    import zlib

    import numpy as np

    out = dict(_drawn_inputs(seed))
    spreads = {}
    factors = {'L0_attn_bln': 8.0}
    for name, (base, spread) in spreads.items():
        noise = np.random.default_rng([zlib.crc32(name.encode()), seed]).standard_normal(out[name].shape)
        drawn = base * np.exp(spread * noise) if base else spread * noise
        out[name] = jnp.asarray(drawn.astype(out[name].dtype))
    for name, factor in factors.items():
        out[name] = (out[name] * factor).astype(out[name].dtype)
    return out
```

```python
from contextlib import ExitStack

import concourse.bass as bass
from concourse import mybir

F32 = mybir.dt.float32
F32R = mybir.dt.float32r
ALU = mybir.AluOpType
ACT = mybir.ActivationFunctionType
AX_X = mybir.AxisListType.X

P = 128
B, N, C = 8, 1024, 256
E, H = 16, 128
M = C // P
T = N // P
GT = 4
GN = GT * P
G = T // GT
STEPS = G * E
LAG = 1
EPS_SUM = 1e-7
EPS_NORM = 1e-12
EPS_LN = 1e-5
LIFT = 2.0 ** 20
WPIECES = 8
WPIECE = 2 * M * E * H // WPIECES

PLAN = {
    0: [("QT", 2)], 1: [("QT", 3)], 2: [("OT", 0)], 3: [("OT", 1), ("Y", 4)],
    4: [("Y", 5), ("XT", 4)], 5: [("Y", 6), ("XT", 5)], 6: [("Y", 7), ("XT", 6)],
    7: [("XT", 7), ("QK", 0)], 8: [("QK", 1)], 9: [("GG", 0), ("LG", 1)], 10: [("QK", 2), ("GG", 1)],
    11: [("QK", 3)], 12: [("GG", 2)], 13: [("QK", 4), ("GG", 3)], 14: [("QK", 5)], 15: [("GG", 4)],
    16: [("QK", 6), ("GG", 5)], 17: [("QK", 7)], 18: [("OT", 0), ("GG", 6)],
    19: [("OT", 1), ("GG", 7), ("KS", 0)], 21: [("QT", 0), ("KV", 0)], 22: [("QT", 1), ("Y", 0)],
    23: [("Y", 1), ("XT", 0)], 24: [("Y", 2), ("XT", 1)], 25: [("Y", 3), ("XT", 2)], 26: [("XT", 3)],
    28: [("LG", 0)],
}
RING_KINDS = ("QT", "Y", "XT", "LG", "OT", "KS", "KV")
SPLIT_XT = {4: 0, 8: 1}
SPLIT_X = {5: 0, 10: 1, 13: 2, 16: 3}
BIAS_X = {9: 0, 14: 1, 28: 2, 29: 3}
SCALE_Q = {19: (0,), 20: (1,), 21: (2, 3), 30: (4, 5), 31: (6, 7)}
FIRST_STEP = min(SPLIT_XT)
LAST_STEPS = 5
PIECE_STEPS = (6, 8, 10, 12, 14, 17, 19, 21)


def batch_offset(kind, a):
    if kind in ("Y", "XT"):
        return int(a < GT)
    if kind == "QT":
        return int(a < T // 4)
    if kind == "LG":
        return 1 - a
    return 1


def stages(it, s):
    out = []
    for kind, a in PLAN.get(s, ()):
        if kind == "OT":
            g = 0 if s >= E else -1
            if 0 <= G * it + g < G * B:
                out.append((kind, a, g))
        elif 0 <= it + batch_offset(kind, a) < B:
            out.append((kind, a, batch_offset(kind, a)))
    return out


def ring_uses():
    return [(it, s, kind, a, off) for it in range(-1, B + 1) for s in range(STEPS)
            if not (it < 0 and s < FIRST_STEP) for kind, a, off in stages(it, s) if kind in RING_KINDS]


RING = ring_uses()
RING_AT = {u[:4]: n for n, u in enumerate(RING)}


def build_program(nc, x, xT, wqk, wvT, wln, b_qk, b_v, b_ln, esel, keys, values, ident_in, out):
    with ExitStack() as ctx:
        def sb(name, shape, dt=F32):
            return ctx.enter_context(nc.sbuf_tensor(name, shape, dt))

        def bank(name):
            return ctx.enter_context(nc.psum_tensor(name, [P, 512], F32))

        def sem(name):
            return ctx.enter_context(nc.semaphore(name))

        keys_h, keys_l = sb("keys_h", [P, M, E, H], F32R), sb("keys_l", [P, M, E, H], F32R)
        vals_h, vals_l = sb("vals_h", [P, E, C], F32R), sb("vals_l", [P, E, C], F32R)
        wqk_h, wqk_l = sb("wqk_h", [P, M, 2 * C], F32R), sb("wqk_l", [P, M, 2 * C], F32R)
        wvl_h, wvl_l = sb("wvl_h", [P, M, C], F32R), sb("wvl_l", [P, M, C], F32R)
        esel_h, esel_l = sb("esel_h", [P, M, P], F32R), sb("esel_l", [P, M, P], F32R)
        qk_bias = sb("qk_bias", [P, 2 * C])
        bvl = sb("bvl", [P, C])
        out_bias = sb("out_bias", [P, C])
        ident = sb("ident", [P, P])
        ones = sb("ones", [P, P])
        eps_ln = sb("eps_ln", [P, 1])

        x_raw = sb("x_raw", [P, T, C])
        xT_raw = sb("xT_raw", [P, M, GN])
        xT_h, xT_l = sb("xT_h", [P, G, M, GN], F32R), sb("xT_l", [P, G, M, GN], F32R)
        x_h, x_l = sb("x_h", [P, 2, C], F32R), sb("x_l", [P, 2, C], F32R)
        qk = sb("qk", [P, 2 * C])
        q2 = sb("q2", [P, T, C])
        q_sum, q4_sum, q_root, q_floor, q_scale = (sb(n, [P, T]) for n in (
            "q_sum", "q4_sum", "q_root", "q_floor", "q_scale"))
        q4_lifted = sb("q4_lifted", [P, T])
        k2, k4 = sb("k2", [P, 2, C]), sb("k4", [P, C])
        k_sum, k_sum_eps, k_scale = (sb(n, [P, 2]) for n in ("k_sum", "k_sum_eps", "k_scale"))
        k2_h, k2_l = sb("k2_h", [P, 2, C], F32R), sb("k2_l", [P, 2, C], F32R)
        k2_total, k4_total = sb("k2_total", [P, C]), sb("k4_total", [P, C])
        col_sums = sb("col_sums", [P, 4, 2])
        col_norm, col_scale = sb("col_norm", [P, M, 2]), sb("col_scale", [P, M, 2])
        gT_h, gT_l = k2_h, k2_l
        kvw_h, kvw_l = sb("kvw_h", [P, M, C], F32R), sb("kvw_l", [P, M, C], F32R)
        qT_h, qT_l = sb("qT_h", [P, 2, 2, M, P], F32R), sb("qT_l", [P, 2, 2, M, P], F32R)
        y = sb("y", [P, 2, C])
        y_stats, y_mv = sb("y_stats", [P, 2, 6]), sb("y_mv", [P, 2, 2])
        y_std, y_rstd = sb("y_std", [P, 2]), sb("y_rstd", [P, 2])
        kvw = y
        x1 = sb("x1", [P, T, C])
        x1T_h, x1T_l = sb("x1T_h", [P, G, M, GN], F32R), sb("x1T_l", [P, G, M, GN], F32R)

        sel = sb("sel", [E, GN])
        sel_rows = sb("sel_rows", [P, E // 4, GN])
        sel_all = sb("sel_all", [P, 2, GN])
        gated = sb("gated", [P, GN])
        gated_h, gated_l = sb("gated_h", [P, 2, GN], F32R), sb("gated_l", [P, 2, GN], F32R)
        oT = sb("oT", [P, M, GN])
        z = sb("z", [P, 2, 2, C])
        z_stats, z_mv = sb("z_stats", [P, 2, 2, 6]), sb("z_mv", [P, 2, 2, 2])
        z_std, z_rstd = sb("z_std", [P, 2, 2]), sb("z_rstd", [P, 2, 2])

        w_stage = [t[:].rearrange("p a n -> p (a n)") for t in (oT, sel_all)]
        wqk_raw = x1[:, 0:4, :].rearrange("p (m a) c -> p m a c", m=M)
        wvT_raw, wln_raw = x1[:, 4:6, :], x1[:, 6:8, :]
        wqk_mean = sb("wqk_mean", [P, 6])
        bqk_raw = z[:, 0, :, :]
        bln_raw = z[:, 1, 0, :]
        bv_col = sb("bv_col", [P, M])
        bv_wide = y[:, 0].rearrange("p (m n) -> p m n", m=M)
        esel_raw = sb("esel_raw", [P, M, E])

        up_bank = [bank("up_bank0"), bank("up_bank1")]
        down_bank = [bank("down_bank0"), bank("down_bank1")]
        qk_bank, g_bank = bank("qk_bank"), bank("g_bank")
        ring_bank = [bank("ring_bank0"), bank("ring_bank1")]

        (w_qk_in, w_v_in, w_ln_in, bias_in, small_in) = map(sem, (
            "w_qk_in", "w_v_in", "w_ln_in", "bias_in", "small_in"))
        piece_in = [sem("piece_in0"), sem("piece_in1")]
        piece_hi, piece_lo = sem("piece_hi"), sem("piece_lo")
        setup_dve, means_made, setup_pe, setup_act, constants_set = map(sem, (
            "setup_dve", "means_made", "setup_pe", "setup_act", "constants_set"))
        x_in, xT_in = [sem("x_in0"), sem("x_in1")], sem("xT_in")
        xT_hi, xT_lo = sem("xT_hi"), sem("xT_lo")
        x_hi, x_lo, x_biased = map(sem, ("x_hi", "x_lo", "x_biased"))
        (qk_projected, qk_biased, q_squared, k_squared, q_fourth, k_eps, k_scaled, k_hi, k_fourth, k_lo,
         k_summed, k4_summed, g_added) = map(sem, (
             "qk_projected", "qk_biased", "q_squared", "k_squared", "q_fourth", "k_eps", "k_scaled",
             "k_hi", "k_fourth", "k_lo", "k_summed", "k4_summed", "g_added"))
        (q_lifted, q_rooted, q_floored, q_max, q_scale_set, g_hi, g_lo, cols_summed, cols_copied,
         cols_rooted, cols_inverted, kv_projected, cols_scaled) = map(sem, (
             "q_lifted", "q_rooted", "q_floored", "q_max", "q_scale_set", "g_hi", "g_lo", "cols_summed",
             "cols_copied", "cols_rooted", "cols_inverted", "kv_projected", "cols_scaled"))
        kv_summed, kv_hi, kv_lo = map(sem, ("kv_summed", "kv_hi", "kv_lo"))
        q_scaled = sem("q_scaled")
        q_transposed, qT_hi, qT_lo = map(sem, ("q_transposed", "qT_hi", "qT_lo"))
        (y_projected, y_added, y_stated, y_aggregated, y_rooted, y_inverted, x1_made, x1_transposed,
         x1T_hi, x1T_lo) = map(sem, (
             "y_projected", "y_added", "y_stated", "y_aggregated", "y_rooted", "y_inverted", "x1_made",
             "x1_transposed", "x1T_hi", "x1T_lo"))
        logits_made, sel_made, rows_in = map(sem, ("logits_made", "sel_made", "rows_in"))
        sel_spread, up_made, gate_applied, gated_hi, gated_lo, down_made = map(sem, (
            "sel_spread", "up_made", "gate_applied", "gated_hi", "gated_lo", "down_made"))
        o_copied = sem("o_copied")
        (o_transposed, z_added, z_stated, z_aggregated, z_rooted, z_inverted, out_made) = map(sem, (
            "o_transposed", "z_added", "z_stated", "z_aggregated", "z_rooted", "z_inverted",
            "out_made"))
        stored = [sem("stored0"), sem("stored1")]
        stood = sem("stood")

        def tile(b, t):
            return b * T + (t + 1)

        def pair(b, p):
            return b * (T // 2) + (p + 1)

        def half(b, h):
            return b * G + (h + 1)

        def out_pair(it, goff, p):
            return it * (2 * G) + (goff * 2 + p + 1)

        def at_least(eng, sm, count):
            if not isinstance(count, int) or count > 0:
                eng.wait_ge(sm, count)

        def stand_at(eng, sm, count):
            at_least(eng, sm, count)
            if not isinstance(count, int):
                eng.sem_inc(stood, 1)

        def ring_place(it, s, kind, a):
            rep = it if isinstance(it, int) else 1
            n = RING_AT[(rep, s, kind, a)]
            if n < 2:
                return ring_bank[n % 2], None, 0
            pit, ps, pkind, pa, poff = RING[n - 2]
            b = it + (pit - rep) + poff
            if pkind == "OT":
                return ring_bank[n % 2], z_added, out_pair(it + (pit - rep), poff, pa)
            read = {"QT": lambda: (qT_lo, pair(b, pa)), "Y": lambda: (y_added, tile(b, pa)),
                    "XT": lambda: (x1T_lo, tile(b, pa)), "LG": lambda: (sel_made, half(b, pa)),
                    "KS": lambda: (cols_copied, b + 1), "KV": lambda: (kv_summed, b * M + M)}[pkind]()
            return (ring_bank[n % 2],) + read

        def ring_of(it, s, kind, a):
            rep = it if isinstance(it, int) else 1
            return ring_bank[RING_AT[(rep, s, kind, a)] % 2]

        def planned(it, s, kinds):
            return [(k, a, off) for k, a, off in stages(it if isinstance(it, int) else 1, s) if k in kinds]

        def has(it, off, lo=0):
            return not isinstance(it, int) or lo <= it + off < B

        def run(eng, step):
            for s in range(FIRST_STEP, STEPS):
                step(-1, s)
            for s in range(STEPS):
                step(0, s)
            with eng.Fori(1, B - 1) as it:
                for s in range(STEPS):
                    step(it, s)
            for s in range(STEPS):
                step(B - 1, s)
            for s in range(LAST_STEPS):
                step(B, s)

        def it_is(it, s, first):
            return isinstance(it, int) and it < 0 and s == first

        def step_exists(it, s, lag=0):
            return not isinstance(it, int) or 0 <= it * STEPS + s - lag < B * STEPS

        def step_no(it, s, lag=0):
            return it * STEPS + (s - lag)

        x_dram = x.rearrange("b (p t) c -> b p t c", t=T)
        out_dram = out.rearrange("b (p t) c -> b p t c", t=T)
        keys_flat = [keys_h[:].rearrange("p m e h -> p (m e h)"), keys_l[:].rearrange("p m e h -> p (m e h)")]
        vals_flat = [vals_h[:].rearrange("p e c -> p (e c)"), vals_l[:].rearrange("p e c -> p (e c)")]

        def piece(i, part):
            flat = keys_flat if i < WPIECES // 2 else vals_flat
            i %= WPIECES // 2
            return flat[part][:, i * WPIECE:(i + 1) * WPIECE]

        block = ctx.enter_context(nc.Block())

        @block.sync
        def _(sp):
            def load_half(it, h):
                at_least(sp, xT_lo, half(it + 1, h) - 1)
                sp.dma_start(xT_raw[:], xT[it + 1, :, h]).then_inc(xT_in, 16)
                at_least(sp, y_added, tile(it, GT * h + GT - 1))
                sp.dma_start(x_raw[:, GT * h:GT * h + GT],
                             x_dram[it + 1, :, GT * h:GT * h + GT]).then_inc(x_in[h], 16)

            def store_pair(it, goff, p):
                at_least(sp, out_made, 2 * out_pair(it, goff, p))
                g = goff % G
                b = it + (goff - g) // G
                t = GT * g + 2 * p
                sp.dma_start(out_dram[b, :, t:t + 2], z[:, p]).then_inc(stored[p], 16)

            def move_rows(it, off, g):
                stand_at(sp, sel_made, half(it + off, g))
                at_least(sp, sel_spread, (it + off) * STEPS + g * E)
                for j in range(4):
                    sp.dma_start(sel_rows[0:P:32, j], sel[j:E:4, :]).then_inc(rows_in, 16)

            sp.dma_start(xT_raw[:], xT[0, :, 0]).then_inc(xT_in, 16)
            sp.dma_start(wqk_raw, wqk).then_inc(w_qk_in, 16)
            sp.dma_start(bqk_raw, b_qk.partition_broadcast(P)).then_inc(bias_in, 16)
            sp.dma_start(x_raw[:, 0:GT], x_dram[0, :, 0:GT]).then_inc(x_in[0], 16)
            sp.dma_start(wvT_raw, wvT).then_inc(w_v_in, 16)
            sp.dma_start(wln_raw, wln).then_inc(w_ln_in, 16)
            for dst, src in ((bln_raw, b_ln.partition_broadcast(P)), (bv_col[:], b_v), (esel_raw[:], esel),
                             (ident[:], ident_in)):
                sp.dma_start(dst, src).then_inc(small_in, 16)
            load_half(-1, 1)
            for i in range(WPIECES):
                if i >= 2:
                    sp.wait_ge(piece_lo, i - 1)
                src = keys if i < WPIECES // 2 else values
                j = i % (WPIECES // 2)
                sp.dma_start(w_stage[i % 2], src[:, j * WPIECE:(j + 1) * WPIECE]).then_inc(piece_in[i % 2], 16)

            def step(it, s):
                if s == 0 and has(it, 1):
                    load_half(it, 0)
                if s == 7 and has(it, 1) and not (isinstance(it, int) and it < 0):
                    load_half(it, 1)
                for kind, a, off in planned(it, s, ("LG", "OT")):
                    if kind == "LG":
                        move_rows(it, off, a)
                    else:
                        store_pair(it, off, a)

            run(sp, step)
            for p in range(2):
                sp.wait_ge(stored[p], 16 * G * B)

        @block.gpsimd
        def _(pool):
            nc.gpsimd.memset(ones[:], 1.0).then_inc(constants_set, 1)
            nc.gpsimd.memset(eps_ln[:], EPS_LN).then_inc(constants_set, 1)
            nc.gpsimd.memset(esel_h[:].bitcast(F32), 0.0).then_inc(constants_set, 1)
            nc.gpsimd.memset(esel_l[:].bitcast(F32), 0.0).then_inc(constants_set, 1)
            for i in range(WPIECES):
                pool.wait_ge(piece_hi, i + 1)
                nc.gpsimd.tensor_tensor(piece(i, 1), w_stage[i % 2], piece(i, 0).bitcast(F32),
                                        ALU.subtract).then_inc(piece_lo, 1)
            def spread_group(grp):
                pool.wait_ge(rows_in, grp * 64 + 64)
                for e in range(E):
                    stand_at(pool, gate_applied, grp * E + (e - 1))
                    i, j = divmod(e, 4)
                    nc.gpsimd.partition_broadcast(sel_all[:, e % 2], sel_rows[32 * i:32 * i + 1, j],
                                                  P).then_inc(sel_spread, 1)

            pool.wait_ge(piece_lo, WPIECES)
            spread_group(0)
            with pool.Fori(1, B * G) as grp:
                spread_group(grp)

        @block.scalar
        def _(act):
            def copy(dst, src, **kw):
                return nc.scalar.activation(dst, src, ACT.Copy, **kw)

            def setup_hi():
                act.wait_ge(setup_dve, 3)
                copy(wqk_h[:], wqk_raw.rearrange("p m a c -> p m (a c)")).then_inc(setup_act, 1)
                act.wait_ge(setup_pe, 1)
                copy(wvl_h[:].rearrange("p m c -> p (m c)"), down_bank[0][:]).then_inc(setup_act, 1)
                act.wait_ge(constants_set, 4)
                act.wait_ge(small_in, 64)
                copy(esel_h[:, :, 0:E], esel_raw[:]).then_inc(setup_act, 1)

            def weights_hi(i):
                act.wait_ge(piece_in[i % 2], 16 * (i // 2 + 1))
                copy(piece(i, 0), w_stage[i % 2]).then_inc(piece_hi, 1)

            def split_hi(it, s):
                if s in SPLIT_XT and has(it, 1):
                    h = SPLIT_XT[s]
                    at_least(act, xT_in, (it + 1) * (16 * G) + 16 * (h + 1))
                    at_least(act, y_projected, tile(it, GT * h + GT - 1))
                    copy(xT_h[:, h], xT_raw[:]).then_inc(xT_hi, 1)
                if s in SPLIT_X and has(it, 1):
                    i = SPLIT_X[s]
                    at_least(act, x_in[i // 2], (it + 1) * 16 + 16)
                    at_least(act, g_added, tile(it + 1, 2 * i - 1))
                    copy(x_h[:], x_raw[:, 2 * i:2 * i + 2]).then_inc(x_hi, 1)

            def squares(b, t):
                n = tile(b, t)
                act.wait_ge(qk_biased, n)
                at_least(act, q_transposed, pair(b - 1, t // 2))
                at_least(act, q_scale_set, b)
                nc.scalar.activation(q2[:, t], qk[:, 0:C], ACT.Square,
                                     accum_out=q_sum[:, t:t + 1]).then_inc(q_squared, 1)
                at_least(act, k_summed, n - 2)
                nc.scalar.activation(k2[:, t % 2], qk[:, C:2 * C], ACT.Square,
                                     accum_out=k_sum[:, t % 2:t % 2 + 1]).then_inc(k_squared, 1)
                act.wait_ge(q_squared, n)
                nc.scalar.activation(qk[:, 0:C], q2[:, t], ACT.Square,
                                     accum_out=q4_sum[:, t:t + 1]).then_inc(q_fourth, 1)

            def k_normalised_hi(b, t):
                n = tile(b, t)
                act.wait_ge(k_scaled, n)
                at_least(act, g_added, n - 2)
                at_least(act, kv_projected, b)
                copy(k2_h[:, t % 2], k2[:, t % 2], scale=k_scale[:, t % 2:t % 2 + 1]).then_inc(k_hi, 1)
                at_least(act, k4_summed, n - 1)
                nc.scalar.activation(k4[:], k2[:, t % 2], ACT.Square,
                                     scale=k_scale[:, t % 2:t % 2 + 1]).then_inc(k_fourth, 1)

            def early(it, s):
                for kind, t, off in planned(it, s - 1, ("QK", "KS")):
                    if kind == "QK":
                        k_normalised_hi(it + off, t)
                        if t == T - 1:
                            act.wait_ge(q_lifted, it + off + 1)
                            nc.scalar.activation(q_root[:], q4_lifted[:], ACT.Sqrt).then_inc(q_rooted, 1)
                    else:
                        act.wait_ge(cols_copied, it + off + 1)
                        nc.scalar.activation(col_norm[:], col_sums[:, 0:M], ACT.Sqrt).then_inc(cols_rooted, 1)

            def late(it, s):
                for kind, a, off in planned(it, s, ("QK", "GG", "KV", "QT", "Y", "XT", "LG", "OT")):
                    b = it + off
                    if kind == "QK":
                        squares(b, a)
                    elif kind == "GG" and a == T - 1:
                        act.wait_ge(g_added, tile(b, a))
                        copy(gT_h[:].rearrange("p m c -> p (m c)"), g_bank[:]).then_inc(g_hi, 1)
                    elif kind == "KV":
                        for m in range(M):
                            act.wait_ge(kv_summed, b * M + m + 1)
                            act.wait_ge(cols_scaled, b + 1)
                            at_least(act, y_projected, b * T)
                            copy(kvw_h[:, m], kvw[:, m], scale=col_scale[:, m, 0:1]).then_inc(kv_hi, 1)
                    elif kind == "QT":
                        act.wait_ge(q_transposed, pair(b, a))
                        at_least(act, y_projected, tile(b, 2 * a - 3))
                        copy(qT_h[:, a % 2].rearrange("p t m n -> p (t m n)"),
                             ring_of(it, s, kind, a)[:]).then_inc(qT_hi, 1)
                    elif kind == "Y":
                        act.wait_ge(y_aggregated, tile(b, a))
                        nc.scalar.activation(y_std[:, a % 2:a % 2 + 1], y_mv[:, a % 2, 1:2], ACT.Sqrt,
                                             bias=eps_ln[:]).then_inc(y_rooted, 1)
                    elif kind == "XT":
                        g, i = divmod(a, GT)
                        act.wait_ge(x1_transposed, tile(b, a))
                        at_least(act, up_made, (b - 1) * STEPS + (g + 1) * E)
                        copy(x1T_h[:, g, :, i * P:(i + 1) * P],
                             ring_of(it, s, kind, a)[:, 0:C].rearrange("p (m n) -> p m n", m=M)
                             ).then_inc(x1T_hi, 1)
                    elif kind == "LG":
                        act.wait_ge(logits_made, half(b, a))
                        at_least(act, rows_in, b * (64 * G) + 64 * a)
                        nc.scalar.activation(sel[:], ring_of(it, s, kind, a)[0:E, :],
                                             ACT.Sigmoid).then_inc(sel_made, 1)
                    elif kind == "OT":
                        n = out_pair(it, off, a)
                        act.wait_ge(z_aggregated, 2 * n)
                        nc.scalar.activation(z_std[:, a], z_mv[:, a, :, 1], ACT.Sqrt,
                                             bias=eps_ln[:]).then_inc(z_rooted, 1)

            def step(it, s):
                early(it, s)
                if step_exists(it, s):
                    f = step_no(it, s)
                    act.wait_ge(gate_applied, f + 1)
                    at_least(act, down_made, f - 1)
                    copy(gated_h[:, s % 2], gated[:]).then_inc(gated_hi, 1)
                late(it, s)
                split_hi(it, s)
                if it_is(it, s, 4):
                    setup_hi()
                if isinstance(it, int) and it < 0 and s in PIECE_STEPS:
                    weights_hi(PIECE_STEPS.index(s))
                if (s - LAG) % E == E - 1 and step_exists(it, s, LAG):
                    f = step_no(it, s, LAG)
                    grp = 2 * it + ((s - LAG) // E)
                    act.wait_ge(down_made, f + 1)
                    at_least(act, o_transposed, 2 * grp)
                    for m in range(M):
                        copy(oT[:, m], down_bank[m][:]).then_inc(o_copied, 1)

            run(act, step)

        @block.vector
        def _(dve):
            V = nc.vector
            dve.wait_ge(w_qk_in, 16)
            dve.wait_ge(bias_in, 16)
            V.tensor_reduce(wqk_mean[:, 0:4], wqk_raw.rearrange("p m a c -> p (m a) c"), AX_X,
                            ALU.add).then_inc(setup_dve, 1)
            V.tensor_reduce(wqk_mean[:, 4:6], bqk_raw, AX_X, ALU.add).then_inc(setup_dve, 1)
            dve.wait_ge(setup_dve, 2)
            wqk_flat = wqk_raw.rearrange("p m a c -> p (m a) c")
            V.tensor_scalar(wqk_mean[:], wqk_mean[:], 1.0 / C, None, ALU.mult).then_inc(means_made, 1)
            dve.wait_ge(means_made, 1)
            for i in range(4):
                last = V.tensor_scalar(wqk_flat[:, i], wqk_flat[:, i], wqk_mean[:, i:i + 1], None, ALU.subtract)
            last.then_inc(setup_dve, 1)
            for a in range(2):
                last = V.tensor_scalar(qk_bias[:, a * C:(a + 1) * C], bqk_raw[:, a], wqk_mean[:, 4 + a:5 + a],
                                       None, ALU.subtract)
            last.then_inc(setup_dve, 1)

            def setup_qk():
                dve.wait_ge(setup_act, 1)
                V.tensor_tensor(wqk_l[:], wqk_raw.rearrange("p m a c -> p m (a c)"), wqk_h[:].bitcast(F32),
                                ALU.subtract).then_inc(setup_dve, 1)
                dve.wait_ge(small_in, 64)
                dve.wait_ge(constants_set, 4)
                for m in range(M):
                    last = V.tensor_scalar(bv_wide[:, m], ones[:], bv_col[:, m:m + 1], None, ALU.mult)
                last.then_inc(setup_dve, 1)
                dve.wait_ge(setup_act, 2)
                V.tensor_tensor(wvl_l[:].rearrange("p m c -> p (m c)"), down_bank[0][:],
                                wvl_h[:].bitcast(F32).rearrange("p m c -> p (m c)"),
                                ALU.subtract).then_inc(setup_dve, 1)

            def setup_rest():
                dve.wait_ge(setup_pe, 2)
                V.tensor_copy(bvl[:], down_bank[1][:, 0:C]).then_inc(setup_dve, 1)
                dve.wait_ge(setup_dve, 8)
                V.tensor_tensor(out_bias[:], bvl[:], bln_raw, ALU.add).then_inc(setup_dve, 1)
                dve.wait_ge(setup_act, 3)
                V.tensor_tensor(esel_l[:, :, 0:E], esel_raw[:], esel_h[:, :, 0:E].bitcast(F32),
                                ALU.subtract).then_inc(setup_dve, 1)
                dve.wait_ge(setup_dve, 10)

            def split_lo(it, s):
                if s - 1 in SPLIT_XT and has(it, 1):
                    h = SPLIT_XT[s - 1]
                    dve.wait_ge(xT_hi, half(it + 1, h))
                    V.tensor_tensor(xT_l[:, h], xT_raw[:], xT_h[:, h].bitcast(F32),
                                    ALU.subtract).then_inc(xT_lo, 1)
                if s - 1 in SPLIT_X and has(it, 1):
                    i = SPLIT_X[s - 1]
                    pair_x = x_raw[:, 2 * i:2 * i + 2]
                    dve.wait_ge(x_hi, pair(it + 1, i))
                    V.tensor_tensor(x_l[:], pair_x, x_h[:].bitcast(F32), ALU.subtract).then_inc(x_lo, 1)
                if s in BIAS_X and has(it, 1):
                    i = BIAS_X[s]
                    pair_x = x_raw[:, 2 * i:2 * i + 2]
                    dve.wait_ge(x_lo, pair(it + 1, i))
                    V.tensor_tensor(pair_x, pair_x, out_bias[:].unsqueeze(1).broadcast_to((P, 2, C)),
                                    ALU.add).then_inc(x_biased, 1)

            def layer_norm(dst, src, mv, rstd):
                return V.tensor_scalar(dst, src, mv[:, 0:1], rstd, ALU.subtract, ALU.mult)

            def early(it, s):
                for kind, a, off in planned(it, s - 1, ("QK", "GG", "KS", "KV", "QT", "Y", "XT", "OT")):
                    b = it + off
                    if kind == "QK":
                        dve.wait_ge(k_squared, tile(b, a))
                        V.tensor_scalar(k_sum_eps[:, a % 2:a % 2 + 1], k_sum[:, a % 2:a % 2 + 1], EPS_SUM,
                                        None, ALU.add).then_inc(k_eps, 1)
                        dve.wait_ge(k_eps, tile(b, a))
                        V.reciprocal(k_scale[:, a % 2:a % 2 + 1],
                                     k_sum_eps[:, a % 2:a % 2 + 1]).then_inc(k_scaled, 1)
                        if a == T - 1:
                            dve.wait_ge(q_fourth, tile(b, a))
                            V.tensor_scalar(q4_lifted[:], q4_sum[:], LIFT * LIFT, 1e-30, ALU.mult,
                                            ALU.max).then_inc(q_lifted, 1)
                            V.tensor_scalar(q_floor[:], q_sum[:], EPS_SUM, EPS_NORM * LIFT, ALU.add,
                                            ALU.mult).then_inc(q_floored, 1)
                    elif kind == "GG" and a == T - 1:
                        dve.wait_ge(g_hi, b + 1)
                        V.tensor_tensor(gT_l[:].rearrange("p m c -> p (m c)"), g_bank[:],
                                        gT_h[:].bitcast(F32).rearrange("p m c -> p (m c)"),
                                        ALU.subtract).then_inc(g_lo, 1)
                    elif kind == "KS":
                        dve.wait_ge(cols_rooted, b + 1)
                        V.reciprocal(col_scale[:], col_norm[:]).then_inc(cols_inverted, 1)
                        dve.wait_ge(cols_inverted, b + 1)
                        V.tensor_scalar(col_scale[:], col_scale[:], float(N) ** -0.5, None,
                                        ALU.mult).then_inc(cols_scaled, 1)
                    elif kind == "KV":
                        for m in range(M):
                            dve.wait_ge(kv_hi, b * M + m + 1)
                            V.scalar_tensor_tensor(out=kvw_l[:, m], in0=kvw[:, m], scalar=col_scale[:, m, 0:1],
                                                   in1=kvw_h[:, m].bitcast(F32), op0=ALU.mult,
                                                   op1=ALU.subtract).then_inc(kv_lo, 1)
                    elif kind == "QT":
                        dve.wait_ge(qT_hi, pair(b, a))
                        V.tensor_tensor(qT_l[:, a % 2].rearrange("p t m n -> p (t m n)"),
                                        ring_of(it, s - 1, kind, a)[:],
                                        qT_h[:, a % 2].bitcast(F32).rearrange("p t m n -> p (t m n)"),
                                        ALU.subtract).then_inc(qT_lo, 1)
                    elif kind == "Y":
                        dve.wait_ge(y_rooted, tile(b, a))
                        V.reciprocal(y_rstd[:, a % 2:a % 2 + 1], y_std[:, a % 2:a % 2 + 1]).then_inc(y_inverted, 1)
                        dve.wait_ge(y_inverted, tile(b, a))
                        at_least(dve, x1_transposed, tile(b - 1, a))
                        layer_norm(x1[:, a], y[:, a % 2], y_mv[:, a % 2],
                                   y_rstd[:, a % 2:a % 2 + 1]).then_inc(x1_made, 1)
                    elif kind == "XT":
                        g, i = divmod(a, GT)
                        dve.wait_ge(x1T_hi, tile(b, a))
                        V.tensor_tensor(x1T_l[:, g, :, i * P:(i + 1) * P],
                                        ring_of(it, s - 1, kind, a)[:, 0:C].rearrange("p (m n) -> p m n", m=M),
                                        x1T_h[:, g, :, i * P:(i + 1) * P].bitcast(F32),
                                        ALU.subtract).then_inc(x1T_lo, 1)
                    elif kind == "OT":
                        n = out_pair(it, off, a)
                        dve.wait_ge(z_rooted, n)
                        V.reciprocal(z_rstd[:, a], z_std[:, a]).then_inc(z_inverted, 1)
                        dve.wait_ge(z_inverted, n)
                        for i in range(2):
                            layer_norm(z[:, a, i], z[:, a, i], z_mv[:, a, i],
                                       z_rstd[:, a, i:i + 1]).then_inc(out_made, 1)

            def late(it, s):
                for kind, a, off in planned(it, s, ("QK",)):
                    dve.wait_ge(qk_projected, tile(it + off, a))
                    at_least(dve, q_fourth, tile(it + off, a) - 1)
                    V.tensor_tensor(qk[:], qk_bank[:], qk_bias[:], ALU.add).then_inc(qk_biased, 1)
                for kind, a, off in planned(it, s - 1, ("QK",)):
                    n = tile(it + off, a)
                    p = a % 2
                    dve.wait_ge(k_hi, n)
                    V.scalar_tensor_tensor(out=k2_l[:, p], in0=k2[:, p], scalar=k_scale[:, p:p + 1],
                                           in1=k2_h[:, p].bitcast(F32), op0=ALU.mult,
                                           op1=ALU.subtract).then_inc(k_lo, 1)
                    if a == 0:
                        at_least(dve, cols_summed, it + off)
                        V.tensor_scalar(k2_total[:], k2[:, p], k_scale[:, p:p + 1], None,
                                        ALU.mult).then_inc(k_summed, 1)
                    else:
                        dve.wait_ge(k_summed, n - 1)
                        V.scalar_tensor_tensor(out=k2_total[:], in0=k2[:, p], scalar=k_scale[:, p:p + 1],
                                               in1=k2_total[:], op0=ALU.mult, op1=ALU.add).then_inc(k_summed, 1)
                    dve.wait_ge(k_fourth, n)
                    if a == 0:
                        V.tensor_copy(k4_total[:], k4[:]).then_inc(k4_summed, 1)
                    else:
                        dve.wait_ge(k4_summed, n - 1)
                        V.tensor_tensor(k4_total[:], k4_total[:], k4[:], ALU.add).then_inc(k4_summed, 1)
                    if a == T - 1:
                        b = it + off
                        dve.wait_ge(q_rooted, b + 1)
                        dve.wait_ge(q_floored, b + 1)
                        V.tensor_tensor(q_root[:], q_root[:], q_floor[:], ALU.max).then_inc(q_max, 1)
                        dve.wait_ge(q_max, b + 1)
                        V.reciprocal(q_scale[:], q_root[:]).then_inc(q_scale_set, 1)
                for kind, a, off in planned(it, s, ("KS", "KV", "Y", "OT")):
                    b = it + off
                    if kind == "KS":
                        dve.wait_ge(cols_summed, b + 1)
                        sums = ring_of(it, s, kind, a)
                        V.tensor_scalar(col_sums[:, 0:M].rearrange("p a b -> p (a b)"), sums[:, 0:2 * M],
                                        EPS_NORM ** 2, None, ALU.max)
                        V.tensor_copy(col_sums[:, M:2 * M].rearrange("p a b -> p (a b)"),
                                      sums[:, 2 * M:4 * M]).then_inc(cols_copied, 1)
                    elif kind == "KV":
                        dve.wait_ge(kv_projected, b + 1)
                        for m in range(M):
                            V.scalar_tensor_tensor(out=kvw[:, m], in0=bvl[:], scalar=col_sums[:, M + m, 0:1],
                                                   in1=ring_of(it, s, kind, a)[:, m * C:(m + 1) * C],
                                                   op0=ALU.mult, op1=ALU.add).then_inc(kv_summed, 1)
                    elif kind == "Y":
                        n = tile(b, a)
                        dve.wait_ge(y_projected, n)
                        dve.wait_ge(x_biased, pair(b, a // 2))
                        V.tensor_tensor(y[:, a % 2], ring_of(it, s, kind, a)[:, 0:C], x_raw[:, a],
                                        ALU.add).then_inc(y_added, 1)
                        dve.wait_ge(y_added, n)
                        V.bn_stats(y_stats[:, a % 2], y[:, a % 2]).then_inc(y_stated, 1)
                        stand_at(dve, y_stated, n)
                        V.bn_aggr(y_mv[:, a % 2], y_stats[:, a % 2]).then_inc(y_aggregated, 1)
                    elif kind == "OT":
                        n = out_pair(it, off, a)
                        t = GT * (off % G) + 2 * a
                        dve.wait_ge(o_transposed, n)
                        at_least(dve, stored[a], it * (16 * G) + off * 16)
                        V.tensor_tensor(z[:, a].rearrange("p t c -> p (t c)"), ring_of(it, s, kind, a)[:],
                                        x1[:, t:t + 2].rearrange("p t c -> p (t c)"),
                                        ALU.add).then_inc(z_added, 1)
                        dve.wait_ge(z_added, n)
                        for i in range(2):
                            V.bn_stats(z_stats[:, a, i], z[:, a, i]).then_inc(z_stated, 1)
                        for i in range(2):
                            stand_at(dve, z_stated, 2 * n - 1 + i)
                            V.bn_aggr(z_mv[:, a, i], z_stats[:, a, i]).then_inc(z_aggregated, 1)
                if s in SCALE_Q and has(it, 1):
                    for t in SCALE_Q[s]:
                        dve.wait_ge(q_scale_set, it + 2)
                        V.tensor_scalar(q2[:, t], q2[:, t], q_scale[:, t:t + 1], LIFT, ALU.mult,
                                        ALU.mult).then_inc(q_scaled, 1)

            def step(it, s):
                early(it, s)
                if it_is(it, s, 9):
                    setup_rest()
                split_lo(it, s)
                if it_is(it, s, 5):
                    setup_qk()
                if step_exists(it, s):
                    f = step_no(it, s)
                    dve.wait_ge(up_made, f + 1)
                    dve.wait_ge(sel_spread, f + 1)
                    at_least(dve, gated_lo, f)
                    V.scalar_tensor_tensor(out=gated[:], in0=up_bank[s % 2][:], scalar=0.0,
                                           in1=sel_all[:, s % 2], op0=ALU.max,
                                           op1=ALU.mult).then_inc(gate_applied, 1)
                late(it, s)
                if step_exists(it, s):
                    dve.wait_ge(gated_hi, f + 1)
                    V.tensor_tensor(gated_l[:, s % 2], gated[:],
                                    gated_h[:, s % 2].bitcast(F32), ALU.subtract).then_inc(gated_lo, 1)

            run(dve, step)

        @block.tensor
        def _(pe):
            mm = nc.tensor.matmul

            def product(dst, pairs, start, stop=True, **kw):
                n = 3 * len(pairs)
                i = 0
                for (lh, ll), (rh, rl) in pairs:
                    for lhs, rhs in ((lh, rh), (lh, rl), (ll, rh)):
                        last = mm(dst, lhs, rhs, start=start and i == 0, stop=stop and i == n - 1, **kw)
                        i += 1
                return last

            def both(hi, lo, *index):
                return hi[index], lo[index]

            pe.wait_ge(w_v_in, 16)
            pe.wait_ge(w_ln_in, 16)
            for c in range(M):
                for m in range(M):
                    last = mm(down_bank[0][:, c * C:(c + 1) * C], wvT_raw[:, m, c * P:(c + 1) * P], wln_raw[:, m],
                              start=(m == 0), stop=(m == M - 1))
            last.then_inc(setup_pe, 1)
            pe.wait_ge(setup_dve, 5)

            ALL = slice(None)

            def layer1(it, s):
                for kind, a, off in planned(it, s, ("QK", "GG", "KS", "KV", "QT", "Y", "XT", "LG", "OT")):
                    b = it + off
                    if kind in RING_KINDS:
                        bk, read, count = ring_place(it, s, kind, a)
                        if read is not None:
                            at_least(pe, read, count)
                    if kind == "QK":
                        h, i = divmod(a, GT)
                        pe.wait_ge(xT_lo, half(b, h))
                        at_least(pe, qk_biased, tile(b, a) - 1)
                        product(qk_bank[:], [(both(xT_h, xT_l, ALL, h, m, slice(i * P, (i + 1) * P)),
                                              both(wqk_h, wqk_l, ALL, m, ALL)) for m in range(M)],
                                start=True).then_inc(qk_projected, 1)
                    elif kind == "GG":
                        pe.wait_ge(k_lo, tile(b, a))
                        pe.wait_ge(x_lo, pair(b, a // 2))
                        if a == 0:
                            at_least(pe, g_lo, b)
                        for m in range(M):
                            last = product(g_bank[:, m * C:(m + 1) * C],
                                           [(both(x_h, x_l, ALL, a % 2, slice(m * P, (m + 1) * P)),
                                             both(k2_h, k2_l, ALL, a % 2, ALL))],
                                           start=(a == 0 and m == 0), stop=(a == T - 1),
                                           skip_group_check=True)
                        last.then_inc(g_added, 1)
                    elif kind == "KS":
                        pe.wait_ge(k_summed, tile(b, T - 1))
                        pe.wait_ge(k4_summed, tile(b, T - 1))
                        for i, total in enumerate((k4_total, k2_total)):
                            for m in range(M):
                                j = 2 * (i * M + m)
                                last = mm(bk[:, j:j + 2], total[:, m * P:(m + 1) * P], ones[:, 0:2],
                                          start=True, stop=True)
                        last.then_inc(cols_summed, 1)
                    elif kind == "KV":
                        pe.wait_ge(g_lo, b + 1)
                        for c in range(M):
                            last = product(bk[:, c * C:(c + 1) * C],
                                           [(both(gT_h, gT_l, ALL, m, slice(c * P, (c + 1) * P)),
                                             both(wvl_h, wvl_l, ALL, m, ALL)) for m in range(M)], start=True)
                        last.then_inc(kv_projected, 1)
                    elif kind == "QT":
                        pe.wait_ge(q_scaled, tile(b, 2 * a + 1))
                        for i in range(2):
                            for m in range(M):
                                j = (i * M + m) * P
                                last = nc.tensor.transpose(bk[:, j:j + P], q2[:, 2 * a + i, m * P:(m + 1) * P],
                                                           ident[:])
                        last.then_inc(q_transposed, 1)
                    elif kind == "Y":
                        h, i = divmod(a, GT)
                        pe.wait_ge(qT_lo, pair(b, a // 2))
                        pe.wait_ge(kv_lo, b * M + M)
                        product(bk[:, 0:C],
                                [(both(xT_h, xT_l, ALL, h, m, slice(i * P, (i + 1) * P)),
                                  both(wvl_h, wvl_l, ALL, m, ALL)) for m in range(M)] +
                                [(both(qT_h, qT_l, ALL, (a // 2) % 2, a % 2, m, ALL),
                                  both(kvw_h, kvw_l, ALL, m, ALL)) for m in range(M)],
                                start=True).then_inc(y_projected, 1)
                    elif kind == "XT":
                        pe.wait_ge(x1_made, tile(b, a))
                        for m in range(M):
                            last = nc.tensor.transpose(bk[:, m * P:(m + 1) * P], x1[:, a, m * P:(m + 1) * P],
                                                       ident[:])
                        last.then_inc(x1_transposed, 1)
                    elif kind == "LG":
                        pe.wait_ge(x1T_lo, tile(b, GT * a + GT - 1))
                        product(bk[:], [(both(esel_h, esel_l, ALL, m, ALL), both(x1T_h, x1T_l, ALL, a, m, ALL))
                                        for m in range(M)], start=True).then_inc(logits_made, 1)
                    elif kind == "OT":
                        n = out_pair(it, off, a)
                        pe.wait_ge(o_copied, n - a - 1 + M)
                        for i in range(2):
                            for m in range(M):
                                j = (i * M + m) * P
                                t = 2 * a + i
                                last = nc.tensor.transpose(bk[:, j:j + P], oT[:, m, t * P:(t + 1) * P], ident[:])
                        last.then_inc(o_transposed, 1)

            def step(it, s):
                if step_exists(it, s):
                    g, e = divmod(s, E)
                    f = step_no(it, s)
                    if e == 0:
                        pe.wait_ge(x1T_lo, tile(it, GT * g + GT - 1))
                        if isinstance(it, int) and it == 0 and g == 0:
                            pe.wait_ge(piece_lo, WPIECES)
                    at_least(pe, gate_applied, f - 1)
                    product(up_bank[s % 2][:], [(both(keys_h, keys_l, ALL, m, e, ALL),
                                                 both(x1T_h, x1T_l, ALL, g, m, ALL)) for m in range(M)],
                            start=True).then_inc(up_made, 1)
                layer1(it, s)
                if it_is(it, s, 7):
                    pe.wait_ge(setup_dve, 6)
                    for m in range(M):
                        last = mm(down_bank[1][:, 0:C], bv_wide[:, m], wln_raw[:, m], start=(m == 0),
                                  stop=(m == M - 1))
                    last.then_inc(setup_pe, 1)
                if it_is(it, s, 20):
                    pe.wait_ge(setup_dve, 10)
                if step_exists(it, s, LAG):
                    e = (s - LAG) % E
                    f = step_no(it, s, LAG)
                    grp = 2 * it + (s - LAG) // E
                    pe.wait_ge(gated_lo, f + 1)
                    if e == 0:
                        at_least(pe, o_copied, M * grp)
                    for c in range(M):
                        r = (s - LAG) % 2
                        last = product(down_bank[c][:], [(both(vals_h, vals_l, ALL, e, slice(c * P, (c + 1) * P)),
                                                          both(gated_h, gated_l, ALL, r, ALL))],
                                       start=(e == 0), stop=(e == E - 1))
                    last.then_inc(down_made, 1)

            run(pe, step)


def kernel(**inputs):
    import numpy as np
    import concourse.bacc as bacc
    from concourse.bass_utils import run_bass_kernel_spmd

    def given(name):
        return np.asarray(inputs["L0_" + name])

    def chunked(w):
        return w.reshape(-1, P, w.shape[-1]).transpose(1, 0, 2)

    x = given("attn_x")
    w = given("attn_Wqkv")
    b = given("attn_bqkv")
    arrays = {
        "x": x,
        "xT": x.reshape(B, P, G, GT, M, P).transpose(0, 5, 2, 4, 3, 1).reshape(B, P, G, M, GN),
        "wqk": chunked(w[:, 0:2 * C]).reshape(P, M, 2, C),
        "wvT": chunked(w[:, 2 * C:].T),
        "wln": chunked(given("attn_Wln")),
        "b_qk": b[0:2 * C].reshape(2, C),
        "b_v": b[2 * C:].reshape(M, P).T,
        "b_ln": given("attn_bln"),
        "esel": chunked(given("ffn_expert_sel").T),
        "keys": given("ffn_keys").reshape(E, M, P, H).transpose(2, 1, 0, 3).reshape(P, M * E * H),
        "values": given("ffn_values").transpose(1, 0, 2).reshape(P, E * C),
        "ident": np.eye(P, dtype=np.float32),
    }
    arrays = {name: np.ascontiguousarray(a) for name, a in arrays.items()}
    nc = bacc.Bacc("TRN2", target_bir_lowering=False, num_devices=1)
    aps = [nc.dram_tensor("in_" + name, a.shape, mybir.dt.from_np(a.dtype), kind="ExternalInput").ap()
           for name, a in arrays.items()]
    out = nc.dram_tensor("out", (B, N, C), F32, kind="ExternalOutput").ap()
    build_program(nc, *aps, out)
    r = run_bass_kernel_spmd(nc, [{"in_" + name: a for name, a in arrays.items()}], core_ids=[0])
    return r.results[0]["out"]
```

```python
from contextlib import ExitStack

import concourse.bass as bass
from concourse import mybir

F32 = mybir.dt.float32
F32R = mybir.dt.float32r
ALU = mybir.AluOpType
ACT = mybir.ActivationFunctionType
AX_X = mybir.AxisListType.X

P = 128
B, N, C = 8, 1024, 256
E, H = 16, 128
M = C // P
T = N // P
GT = 4
GN = GT * P
G = T // GT
STEPS = G * E
LAG = 1
LOW = 32
EPS_SUM = 1e-7
EPS_NORM = 1e-12
EPS_LN = 1e-5
LIFT = 2.0 ** 20
WPIECES = 8
WPIECE = 2 * M * E * H // WPIECES

LOOP = dict(
    plan={
        0: [("QT", 2)], 1: [("QT", 3)], 2: [("OT", 0)], 3: [("OT", 1), ("Y", 4)],
        4: [("Y", 5)], 5: [("Y", 6), ("XT", 4)], 6: [("Y", 7), ("XT", 5)],
        7: [("XT", 6), ("QK", 0)], 8: [("XT", 7), ("QK", 1)], 9: [("GG", 0)], 10: [("QK", 2), ("GG", 1), ("LG", 1)],
        11: [("QK", 3)], 12: [("GG", 2)], 13: [("QK", 4), ("GG", 3)], 14: [("QK", 5)], 15: [("GG", 4)],
        16: [("QK", 6), ("GG", 5)], 17: [("QK", 7)], 18: [("OT", 0), ("GG", 6)],
        19: [("GG", 7), ("KS", 0)], 20: [("OT", 1)], 21: [("QT", 0), ("KV", 0)], 22: [("QT", 1)], 23: [("Y", 0)],
        24: [("Y", 1), ("XT", 0)], 25: [("Y", 2), ("XT", 1)], 26: [("Y", 3), ("XT", 2)], 27: [("XT", 3)],
        28: [("LG", 0)],
    },
    split_xT={4: 0, 8: 1},
    split_x={5: 0, 10: 1, 13: 2, 16: 3},
    bias_x={9: 0, 14: 1, 28: 2, 29: 3},
    scale_q={19: (0,), 20: (1,), 21: (2, 3), 30: (4, 5), 31: (6, 7)})
FIRST = dict(
    plan={
        7: [("QK", 0)], 8: [("QK", 1)], 9: [("QK", 2), ("GG", 0)], 10: [("QK", 3), ("GG", 1)],
        11: [("QK", 4), ("GG", 2)], 12: [("QK", 5), ("GG", 3)], 13: [("QK", 6), ("GG", 4)],
        14: [("QK", 7), ("GG", 5)], 15: [("GG", 6), ("GG", 7)], 16: [("KS", 0), ("QT", 0)],
        17: [("KV", 0), ("QT", 1)], 18: [("Y", 0)], 19: [("Y", 1), ("XT", 0)], 20: [("Y", 2), ("XT", 1)],
        21: [("Y", 3), ("XT", 2)], 22: [("XT", 3)], 23: [("LG", 0)],
    },
    split_xT={4: 0, 9: 1}, split_x={5: 0, 9: 1, 11: 2, 13: 3}, bias_x={17: 0, 18: 1, 25: 2, 26: 3},
    scale_q={15: (0, 1), 16: (2, 3), 24: (4, 5, 6, 7)})
RING_KINDS = ("QT", "Y", "XT", "LG", "OT", "KS", "KV")
FIRST_STEP = min(FIRST["split_xT"])
LAST_STEPS = 5
PIECE_STEPS = ((-1, 9), (-1, 12), (-1, 15), (-1, 17), (0, 1), (0, 3), (0, 5), (0, 7))
PIECE_LOADS = ((-1, 14), (-1, 15), (-1, 17), (-1, 18), (0, 2), (0, 3))


def batch_offset(kind, a):
    if kind in ("Y", "XT"):
        return int(a < GT)
    if kind == "QT":
        return int(a < T // 4)
    if kind == "LG":
        return 1 - a
    return 1


def schedule(it):
    return FIRST if isinstance(it, int) and it < 0 else LOOP


def stages(it, s):
    out = []
    for kind, a in schedule(it)["plan"].get(s, ()):
        if kind == "OT":
            g = 0 if s >= E else -1
            if 0 <= G * it + g < G * B:
                out.append((kind, a, g))
        elif 0 <= it + batch_offset(kind, a) < B:
            out.append((kind, a, batch_offset(kind, a)))
    return out


def ring_uses():
    return [(it, s, kind, a, off) for it in range(-1, B + 1) for s in range(STEPS)
            if not (it < 0 and s < FIRST_STEP) for kind, a, off in stages(it, s) if kind in RING_KINDS]


RING = ring_uses()
RING_AT = {u[:4]: n for n, u in enumerate(RING)}


def build_program(nc, x, xT, wqk, wvT, wln, b_qk, b_v, b_ln, esel, keys, values, ident_in, out):
    with ExitStack() as ctx:
        def sb(name, shape, dt=F32):
            return ctx.enter_context(nc.sbuf_tensor(name, shape, dt))

        def bank(name):
            return ctx.enter_context(nc.psum_tensor(name, [P, 512], F32))

        def sem(name):
            return ctx.enter_context(nc.semaphore(name))

        keys_h, keys_l = sb("keys_h", [P, E, M, H], F32R), sb("keys_l", [P, E, M, H], F32R)
        vals_h, vals_l = sb("vals_h", [P, E, C], F32R), sb("vals_l", [P, E, C], F32R)
        wqk_h, wqk_l = sb("wqk_h", [P, M, 2 * C], F32R), sb("wqk_l", [P, M, 2 * C], F32R)
        wvl_h, wvl_l = sb("wvl_h", [P, M, C], F32R), sb("wvl_l", [P, M, C], F32R)
        esel_h, esel_hl = sb("esel_h", [P, M, P], F32R), sb("esel_hl", [P, M, P], F32R)
        qk_bias = sb("qk_bias", [P, 2 * C])
        bvl = sb("bvl", [P, C])
        out_bias = sb("out_bias", [P, C])
        ident = sb("ident", [P, P])
        ones = sb("ones", [P, P])
        eps_ln = sb("eps_ln", [P, 1])

        x_raw = sb("x_raw", [P, T, C])
        xT_raw = sb("xT_raw", [P, M, GN])
        xT_h, xT_l = sb("xT_h", [P, G, M, GN], F32R), sb("xT_l", [P, G, M, GN], F32R)
        x_h, x_l = sb("x_h", [P, 2, C], F32R), sb("x_l", [P, 2, C], F32R)
        qk = sb("qk", [P, 2 * C])
        q2 = sb("q2", [P, T, C])
        q_sum, q4_sum, q_root, q_floor, q_scale = (sb(n, [P, T]) for n in (
            "q_sum", "q4_sum", "q_root", "q_floor", "q_scale"))
        q4_lifted = sb("q4_lifted", [P, T])
        k2, k4 = sb("k2", [P, 2, C]), sb("k4", [P, C])
        k_sum, k_sum_eps, k_scale = (sb(n, [P, 2]) for n in ("k_sum", "k_sum_eps", "k_scale"))
        k2_h, k2_l = sb("k2_h", [P, 2, C], F32R), sb("k2_l", [P, 2, C], F32R)
        k2_total, k4_total = sb("k2_total", [P, C]), sb("k4_total", [P, C])
        col_sums = sb("col_sums", [P, 4, 2])
        col_norm, col_scale = sb("col_norm", [P, M, 2]), sb("col_scale", [P, M, 2])
        gT_h, gT_l = k2_h, k2_l
        kvw_h, kvw_l = sb("kvw_h", [P, M, C], F32R), sb("kvw_l", [P, M, C], F32R)
        qT_h, qT_l = sb("qT_h", [P, 2, 2, M, P], F32R), sb("qT_l", [P, 2, 2, M, P], F32R)
        y = sb("y", [P, 2, C])
        y_stats, y_mv = sb("y_stats", [P, 2, 6]), sb("y_mv", [P, 2, 2])
        y_std, y_rstd = sb("y_std", [P, 2]), sb("y_rstd", [P, 2])
        kvw = y
        x1 = sb("x1", [P, T, C])
        x1T_h, x1T_l = sb("x1T_h", [P, G, M, GN], F32R), sb("x1T_l", [P, G, M, GN], F32R)

        sel = sb("sel", [E, GN])
        sel_rows = sb("sel_rows", [P, E // 4, GN])
        sel_all = sb("sel_all", [P, 2, GN])
        gated = sb("gated", [P, GN])
        gated_h, gated_l = sb("gated_h", [P, 2, GN], F32R), sb("gated_l", [P, 2, GN], F32R)
        oT = sb("oT", [P, M, GN])
        z = sb("z", [P, 2, 2, C])
        z_stats, z_mv = sb("z_stats", [P, 2, 2, 6]), sb("z_mv", [P, 2, 2, 2])
        z_std, z_rstd, z_shift = (sb(n, [P, 2, 2]) for n in ("z_std", "z_rstd", "z_shift"))

        w_stage = [oT[:].rearrange("p a n -> p (a n)"), z[:].rearrange("p a t c -> p (a t c)")]
        wqk_raw = x1[:, 0:4, :].rearrange("p (m a) c -> p m a c", m=M)
        wvT_raw, wln_raw = x1[:, 4:6, :], x1[:, 6:8, :]
        wqk_flat = wqk_raw.rearrange("p m a c -> p (m a) c")
        wqk_hi_flat = wqk_h[:].rearrange("p m (a c) -> p (m a) c", a=2)
        wqk_lo_flat = wqk_l[:].rearrange("p m (a c) -> p (m a) c", a=2)
        minus_mean, bias_mean = sb("minus_mean", [P, 2 * M]), sb("bias_mean", [P, 2])
        bqk_raw = sel_all[:, 0].rearrange("p (a c) -> p a c", a=2)
        bln_raw = y[:, 1]
        bv_col = sb("bv_col", [P, M])
        bv_wide = y[:, 0].rearrange("p (m n) -> p m n", m=M)
        table_ahead = sb("table_ahead", [P, 1])
        esel_raw = sb("esel_raw", [P, M, E])

        up_bank = [bank("up_bank0"), bank("up_bank1")]
        down_bank = [bank("down_bank0"), bank("down_bank1")]
        qk_bank, g_bank = bank("qk_bank"), bank("g_bank")
        ring_bank = [bank("ring_bank0"), bank("ring_bank1")]

        (w_qk_in, w_v_in, w_ln_in, bias_in, small_in) = map(sem, (
            "w_qk_in", "w_v_in", "w_ln_in", "bias_in", "small_in"))
        piece_in = [sem("piece_in0"), sem("piece_in1")]
        piece_hi, piece_lo = sem("piece_hi"), sem("piece_lo")
        (constants_set, wqk_summed, wqk_mean_set, wqk_hi, wqk_lo, bias_summed, bias_mean_set, qk_bias_set,
         bv_spread, wvl_made, wvl_hi, wvl_lo, esel_hi, esel_lo, bvl_made, bvl_copied, out_bias_set) = map(sem, (
             "constants_set", "wqk_summed", "wqk_mean_set", "wqk_hi", "wqk_lo", "bias_summed",
             "bias_mean_set", "qk_bias_set", "bv_spread", "wvl_made", "wvl_hi", "wvl_lo", "esel_hi",
             "esel_lo", "bvl_made", "bvl_copied", "out_bias_set"))
        x_in, xT_in = [sem("x_in0"), sem("x_in1")], sem("xT_in")
        xT_hi, xT_lo = sem("xT_hi"), sem("xT_lo")
        x_hi, x_lo, x_biased = map(sem, ("x_hi", "x_lo", "x_biased"))
        (qk_projected, qk_biased, q_squared, k_squared, q_fourth, k_eps, k_scaled, k_hi, k_fourth, k_lo,
         k_summed, k4_summed, g_added) = map(sem, (
             "qk_projected", "qk_biased", "q_squared", "k_squared", "q_fourth", "k_eps", "k_scaled",
             "k_hi", "k_fourth", "k_lo", "k_summed", "k4_summed", "g_added"))
        (q_lifted, q_rooted, q_floored, q_max, q_scale_set, g_hi, g_lo, cols_summed, cols_copied,
         cols_rooted, cols_inverted, kv_projected, cols_scaled) = map(sem, (
             "q_lifted", "q_rooted", "q_floored", "q_max", "q_scale_set", "g_hi", "g_lo", "cols_summed",
             "cols_copied", "cols_rooted", "cols_inverted", "kv_projected", "cols_scaled"))
        kv_summed, kv_hi, kv_lo = map(sem, ("kv_summed", "kv_hi", "kv_lo"))
        q_scaled = sem("q_scaled")
        q_transposed, qT_hi, qT_lo = map(sem, ("q_transposed", "qT_hi", "qT_lo"))
        (y_projected, y_added, y_stated, y_aggregated, y_rooted, y_inverted, x1_made, x1_transposed,
         x1T_hi, x1T_lo) = map(sem, (
             "y_projected", "y_added", "y_stated", "y_aggregated", "y_rooted", "y_inverted", "x1_made",
             "x1_transposed", "x1T_hi", "x1T_lo"))
        logits_made, logits_low, logits_summed, sel_made = map(sem, (
            "logits_made", "logits_low", "logits_summed", "sel_made"))
        rows_in = [sem("rows_in%d" % j) for j in range(4)]
        sel_spread, up_made, gate_applied, gated_hi, gated_lo, down_made = map(sem, (
            "sel_spread", "up_made", "gate_applied", "gated_hi", "gated_lo", "down_made"))
        o_copied = sem("o_copied")
        (o_transposed, z_added, z_stated, z_aggregated, z_rooted, z_inverted, z_shift_made, out_made) = map(sem, (
            "o_transposed", "z_added", "z_stated", "z_aggregated", "z_rooted", "z_inverted",
            "z_shift_made", "out_made"))
        stored = [sem("stored0"), sem("stored1")]
        stood = sem("stood")

        def tile(b, t):
            return b * T + (t + 1)

        def pair(b, p):
            return b * (T // 2) + (p + 1)

        def half(b, h):
            return b * G + (h + 1)

        def out_pair(it, goff, p):
            return it * (2 * G) + (goff * 2 + p + 1)

        def at_least(eng, sm, count):
            if not isinstance(count, int) or count > 0:
                eng.wait_ge(sm, count)

        def stand_at(eng, sm, count):
            at_least(eng, sm, count)
            if not isinstance(count, int):
                eng.sem_inc(stood, 1)

        def ring_place(it, s, kind, a):
            rep = it if isinstance(it, int) else 1
            n = RING_AT[(rep, s, kind, a)]
            if n < 2:
                return ring_bank[n % 2], None, 0
            pit, ps, pkind, pa, poff = RING[n - 2]
            b = it + (pit - rep) + poff
            if pkind == "OT":
                return ring_bank[n % 2], z_added, out_pair(it + (pit - rep), poff, pa)
            read = {"QT": lambda: (qT_lo, pair(b, pa)), "Y": lambda: (y_added, tile(b, pa)),
                    "XT": lambda: (x1T_lo, tile(b, pa)), "LG": lambda: (logits_summed, half(b, pa)),
                    "KS": lambda: (cols_copied, b + 1), "KV": lambda: (kv_summed, b * M + M)}[pkind]()
            return (ring_bank[n % 2],) + read

        def ring_of(it, s, kind, a):
            rep = it if isinstance(it, int) else 1
            return ring_bank[RING_AT[(rep, s, kind, a)] % 2]

        def planned(it, s, kinds):
            return [(k, a, off) for k, a, off in stages(it if isinstance(it, int) else 1, s) if k in kinds]

        def transposed_first(planned_stages):
            return sorted(planned_stages, key=lambda stage: stage[0] != "XT")

        def has(it, off, lo=0):
            return not isinstance(it, int) or lo <= it + off < B

        def run(eng, step):
            for s in range(FIRST_STEP, STEPS):
                step(-1, s)
            for s in range(STEPS):
                step(0, s)
            with eng.Fori(1, B - 1) as it:
                for s in range(STEPS):
                    step(it, s)
            for s in range(STEPS):
                step(B - 1, s)
            for s in range(LAST_STEPS):
                step(B, s)

        def it_is(it, s, first):
            return isinstance(it, int) and it < 0 and s == first

        def step_exists(it, s, lag=0):
            return not isinstance(it, int) or 0 <= it * STEPS + s - lag < B * STEPS

        def step_no(it, s, lag=0):
            return it * STEPS + (s - lag)

        x_dram = x.rearrange("b (p t) c -> b p t c", t=T)
        out_dram = out.rearrange("b (p t) c -> b p t c", t=T)
        keys_flat = [keys_h[:].rearrange("p e m h -> p (e m h)"), keys_l[:].rearrange("p e m h -> p (e m h)")]
        vals_flat = [vals_h[:].rearrange("p e c -> p (e c)"), vals_l[:].rearrange("p e c -> p (e c)")]

        def piece(i, part):
            flat = (keys_flat, vals_flat)[i % 2]
            return flat[part][:, (i // 2) * WPIECE:(i // 2 + 1) * WPIECE]

        def first_group(it, g):
            return isinstance(it, int) and it == 0 and g == 0

        block = ctx.enter_context(nc.Block())

        @block.sync
        def _(sp):
            def load_half(it, h):
                at_least(sp, xT_lo, half(it + 1, h) - 1)
                sp.dma_start(xT_raw[:], xT[it + 1, :, h]).then_inc(xT_in, 16)
                at_least(sp, y_added, tile(it, GT * h + GT - 1))
                sp.dma_start(x_raw[:, GT * h:GT * h + GT],
                             x_dram[it + 1, :, GT * h:GT * h + GT]).then_inc(x_in[h], 16)

            def load_piece(i):
                src = (keys, values)[i % 2]
                sp.dma_start(w_stage[i % 2], src[:, (i // 2) * WPIECE:(i // 2 + 1) * WPIECE]
                             ).then_inc(piece_in[i % 2], 16)

            def store_pair(it, goff, p):
                at_least(sp, out_made, 2 * out_pair(it, goff, p))
                g = goff % G
                b = it + (goff - g) // G
                t = GT * g + 2 * p
                sp.dma_start(out_dram[b, :, t:t + 2], z[:, p]).then_inc(stored[p], 16)

            def move_rows(it, off, g):
                stand_at(sp, sel_made, half(it + off, g))
                at_least(sp, sel_spread, (it + off) * STEPS + g * E)
                for j in (1, 2, 3, 0):
                    sp.dma_start(sel_rows[0:P:32, j], sel[j:E:4, :]).then_inc(rows_in[j], 16)

            sp.dma_start(xT_raw[:], xT[0, :, 0]).then_inc(xT_in, 16)
            sp.dma_start(wqk_raw, wqk).then_inc(w_qk_in, 16)
            sp.dma_start(bqk_raw, b_qk.partition_broadcast(P)).then_inc(bias_in, 16)
            sp.dma_start(x_raw[:, 0:GT], x_dram[0, :, 0:GT]).then_inc(x_in[0], 16)
            sp.dma_start(wvT_raw, wvT).then_inc(w_v_in, 16)
            sp.dma_start(wln_raw, wln).then_inc(w_ln_in, 16)
            for dst, src in ((bln_raw, b_ln.partition_broadcast(P)), (bv_col[:], b_v), (esel_raw[:], esel),
                             (ident[:], ident_in)):
                sp.dma_start(dst, src).then_inc(small_in, 16)
            load_half(-1, 1)
            for i in range(2):
                load_piece(i)

            def step(it, s):
                if isinstance(it, int) and (it, s) in PIECE_LOADS:
                    i = 2 + PIECE_LOADS.index((it, s))
                    sp.wait_ge(piece_lo, i - 1)
                    load_piece(i)
                if s == 0 and has(it, 1):
                    load_half(it, 0)
                if s == 7 and has(it, 1) and not (isinstance(it, int) and it < 0):
                    load_half(it, 1)
                for kind, a, off in planned(it, s, ("LG", "OT")):
                    if kind == "LG":
                        move_rows(it, off, a)
                    else:
                        store_pair(it, off, a)

            run(sp, step)
            for p in range(2):
                sp.wait_ge(stored[p], 16 * G * B)

        @block.gpsimd
        def _(pool):
            nc.gpsimd.memset(ones[:], 1.0).then_inc(constants_set, 1)
            nc.gpsimd.memset(eps_ln[:], EPS_LN).then_inc(constants_set, 1)
            nc.gpsimd.memset(esel_h[:].bitcast(F32), 0.0).then_inc(constants_set, 1)
            nc.gpsimd.memset(esel_hl[:].bitcast(F32), 0.0).then_inc(constants_set, 1)
            def weights_lo(i):
                pool.wait_ge(piece_hi, i + 1)
                nc.gpsimd.tensor_tensor(piece(i, 1), w_stage[i % 2], piece(i, 0).bitcast(F32),
                                        ALU.subtract).then_inc(piece_lo, 1)

            for i in range(WPIECES):
                if PIECE_STEPS[i][0] < 0:
                    weights_lo(i)

            def spread_group(grp):
                for e in range(E):
                    stand_at(pool, gate_applied, grp * E + (e - 1))
                    i, j = divmod(e, 4)
                    if e == 0:
                        stand_at(pool, sel_made, grp + 1)
                        row = sel[0:1, :]
                    else:
                        if e <= 4:
                            stand_at(pool, rows_in[j], grp * 16 + 16)
                        row = sel_rows[32 * i:32 * i + 1, j]
                    nc.gpsimd.partition_broadcast(sel_all[:, e % 2], row, P).then_inc(sel_spread, 1)
                    if isinstance(grp, int) and grp == 0 and (0, e - 2) in PIECE_STEPS:
                        i = PIECE_STEPS.index((0, e - 2))
                        pool.wait_ge(sel_spread, e + 1)
                        weights_lo(i)
                        pool.wait_ge(piece_lo, i + 1)

            pool.wait_ge(qk_bias_set, 2)
            spread_group(0)
            with pool.Fori(1, B * G) as grp:
                spread_group(grp)

        @block.scalar
        def _(act):
            def copy(dst, src, **kw):
                return nc.scalar.activation(dst, src, ACT.Copy, **kw)

            def wqk_split_hi():
                act.wait_ge(wqk_mean_set, 1)
                for i in range(2 * M):
                    nc.scalar.activation(wqk_hi_flat[:, i], wqk_flat[:, i], ACT.Identity,
                                         bias=minus_mean[:, i:i + 1]).then_inc(wqk_hi, 1)

            def wvl_esel_hi():
                act.wait_ge(wvl_made, 1)
                copy(wvl_h[:].rearrange("p m c -> p (m c)"), down_bank[0][:]).then_inc(wvl_hi, 1)
                act.wait_ge(constants_set, 4)
                act.wait_ge(small_in, 64)
                copy(esel_hl[:, :, 0:E], esel_raw[:])
                copy(esel_h[:, :, 0:E], esel_raw[:]).then_inc(esel_hi, 1)

            def weights_hi(i):
                act.wait_ge(piece_in[i % 2], 16 * (i // 2 + 1))
                copy(piece(i, 0), w_stage[i % 2]).then_inc(piece_hi, 1)

            def split_hi(it, s):
                sch = schedule(it)
                if s in sch["split_xT"] and has(it, 1):
                    h = sch["split_xT"][s]
                    at_least(act, xT_in, (it + 1) * (16 * G) + 16 * (h + 1))
                    at_least(act, y_projected, tile(it, GT * h + GT - 1))
                    copy(xT_h[:, h], xT_raw[:]).then_inc(xT_hi, 1)
                if s in sch["split_x"] and has(it, 1):
                    i = sch["split_x"][s]
                    at_least(act, x_in[i // 2], (it + 1) * 16 + 16)
                    at_least(act, g_added, tile(it + 1, 2 * i - 1))
                    copy(x_h[:], x_raw[:, 2 * i:2 * i + 2]).then_inc(x_hi, 1)

            def squares(b, t):
                n = tile(b, t)
                act.wait_ge(qk_biased, n)
                at_least(act, q_transposed, pair(b - 1, t // 2))
                at_least(act, q_scale_set, b)
                nc.scalar.activation(q2[:, t], qk[:, 0:C], ACT.Square,
                                     accum_out=q_sum[:, t:t + 1]).then_inc(q_squared, 1)
                at_least(act, k_summed, n - 2)
                nc.scalar.activation(k2[:, t % 2], qk[:, C:2 * C], ACT.Square,
                                     accum_out=k_sum[:, t % 2:t % 2 + 1]).then_inc(k_squared, 1)
                act.wait_ge(q_squared, n)
                nc.scalar.activation(qk[:, 0:C], q2[:, t], ACT.Square,
                                     accum_out=q4_sum[:, t:t + 1]).then_inc(q_fourth, 1)

            def k_normalised_hi(b, t):
                n = tile(b, t)
                act.wait_ge(k_scaled, n)
                at_least(act, g_added, n - 2)
                at_least(act, kv_projected, b)
                copy(k2_h[:, t % 2], k2[:, t % 2], scale=k_scale[:, t % 2:t % 2 + 1]).then_inc(k_hi, 1)
                at_least(act, k4_summed, n - 1)
                nc.scalar.activation(k4[:], k2[:, t % 2], ACT.Square,
                                     scale=k_scale[:, t % 2:t % 2 + 1]).then_inc(k_fourth, 1)

            def early(it, s):
                for kind, t, off in planned(it, s - 1, ("QK", "KS", "LG")):
                    if kind == "LG":
                        act.wait_ge(logits_summed, half(it + off, t))
                        nc.scalar.activation(sel[:], sel[:], ACT.Sigmoid).then_inc(sel_made, 1)
                    elif kind == "QK":
                        k_normalised_hi(it + off, t)
                        if t == T - 1:
                            act.wait_ge(q_lifted, it + off + 1)
                            nc.scalar.activation(q_root[:], q4_lifted[:], ACT.Sqrt).then_inc(q_rooted, 1)
                    else:
                        act.wait_ge(cols_copied, it + off + 1)
                        nc.scalar.activation(col_norm[:], col_sums[:, 0:M], ACT.Sqrt).then_inc(cols_rooted, 1)

            def late(it, s):
                for kind, a, off in planned(it, s - 1, ("OT",)):
                    n = out_pair(it, off, a)
                    act.wait_ge(z_shift_made, n)
                    for i in range(2):
                        nc.scalar.activation(z[:, a, i], z[:, a, i], ACT.Identity, bias=z_shift[:, a, i:i + 1],
                                             scale=z_rstd[:, a, i:i + 1]).then_inc(out_made, 1)
                for kind, a, off in transposed_first(
                        planned(it, s, ("QK", "GG", "KV", "QT", "Y", "XT", "LG", "OT"))):
                    b = it + off
                    if kind == "QK":
                        squares(b, a)
                    elif kind == "GG" and a == T - 1:
                        act.wait_ge(g_added, tile(b, a))
                        copy(gT_h[:].rearrange("p m c -> p (m c)"), g_bank[:]).then_inc(g_hi, 1)
                    elif kind == "KV":
                        for m in range(M):
                            act.wait_ge(kv_summed, b * M + m + 1)
                            act.wait_ge(cols_scaled, b + 1)
                            at_least(act, y_projected, b * T)
                            copy(kvw_h[:, m], kvw[:, m], scale=col_scale[:, m, 0:1]).then_inc(kv_hi, 1)
                    elif kind == "QT":
                        act.wait_ge(q_transposed, pair(b, a))
                        at_least(act, y_projected, tile(b, 2 * a - 3))
                        copy(qT_h[:, a % 2].rearrange("p t m n -> p (t m n)"),
                             ring_of(it, s, kind, a)[:]).then_inc(qT_hi, 1)
                    elif kind == "Y":
                        act.wait_ge(y_aggregated, tile(b, a))
                        nc.scalar.activation(y_std[:, a % 2:a % 2 + 1], y_mv[:, a % 2, 1:2], ACT.Sqrt,
                                             bias=eps_ln[:]).then_inc(y_rooted, 1)
                    elif kind == "XT":
                        g, i = divmod(a, GT)
                        act.wait_ge(x1_transposed, tile(b, a))
                        at_least(act, up_made, (b - 1) * STEPS + (g + 1) * E)
                        copy(x1T_h[:, g, :, i * P:(i + 1) * P],
                             ring_of(it, s, kind, a)[:, 0:C].rearrange("p (m n) -> p m n", m=M)
                             ).then_inc(x1T_hi, 1)
                    elif kind == "LG":
                        act.wait_ge(logits_made, half(b, a))
                        for j in range(4):
                            at_least(act, rows_in[j], b * (16 * G) + 16 * a)
                        at_least(act, sel_spread, b * STEPS + a * E - (E - 1))
                        copy(sel[:], ring_of(it, s, kind, a)[LOW:LOW + E, :]).then_inc(logits_low, 1)
                    elif kind == "OT":
                        n = out_pair(it, off, a)
                        act.wait_ge(z_aggregated, 2 * n)
                        nc.scalar.activation(z_std[:, a], z_mv[:, a, :, 1], ACT.Sqrt,
                                             bias=eps_ln[:]).then_inc(z_rooted, 1)

            def step(it, s):
                early(it, s)
                if step_exists(it, s):
                    f = step_no(it, s)
                    act.wait_ge(gate_applied, f + 1)
                    at_least(act, down_made, f - 1)
                    copy(gated_h[:, s % 2], gated[:]).then_inc(gated_hi, 1)
                late(it, s)
                split_hi(it, s)
                if it_is(it, s, 22):
                    act.wait_ge(constants_set, 4)
                    nc.scalar.activation(table_ahead[:], eps_ln[:], ACT.Sigmoid)
                if it_is(it, s, 4):
                    wqk_split_hi()
                if it_is(it, s, 9):
                    wvl_esel_hi()
                if isinstance(it, int) and (it, s) in PIECE_STEPS:
                    weights_hi(PIECE_STEPS.index((it, s)))
                if (s - LAG) % E == E - 1 and step_exists(it, s, LAG):
                    f = step_no(it, s, LAG)
                    grp = 2 * it + ((s - LAG) // E)
                    act.wait_ge(down_made, f + 1)
                    at_least(act, o_transposed, 2 * grp)
                    if first_group(it, (s - LAG) // E):
                        act.wait_ge(piece_lo, WPIECES)
                    for m in range(M):
                        copy(oT[:, m], down_bank[m][:]).then_inc(o_copied, 1)

            run(act, step)

        @block.vector
        def _(dve):
            V = nc.vector

            def wqk_split_lo():
                dve.wait_ge(w_qk_in, 16)
                V.tensor_reduce(minus_mean[:], wqk_flat, AX_X, ALU.add).then_inc(wqk_summed, 1)
                dve.wait_ge(wqk_summed, 1)
                V.tensor_scalar(minus_mean[:], minus_mean[:], -1.0 / C, None, ALU.mult).then_inc(wqk_mean_set, 1)
                dve.wait_ge(wqk_mean_set, 1)
                for i in range(2 * M):
                    dve.wait_ge(wqk_hi, i + 1)
                    V.scalar_tensor_tensor(out=wqk_lo_flat[:, i], in0=wqk_flat[:, i], scalar=minus_mean[:, i:i + 1],
                                           in1=wqk_hi_flat[:, i].bitcast(F32), op0=ALU.add,
                                           op1=ALU.subtract).then_inc(wqk_lo, 1)
                dve.wait_ge(bias_in, 16)
                V.tensor_reduce(bias_mean[:], bqk_raw, AX_X, ALU.add).then_inc(bias_summed, 1)
                dve.wait_ge(bias_summed, 1)
                V.tensor_scalar(bias_mean[:], bias_mean[:], 1.0 / C, None, ALU.mult).then_inc(bias_mean_set, 1)
                dve.wait_ge(bias_mean_set, 1)
                for a in range(2):
                    V.tensor_scalar(qk_bias[:, a * C:(a + 1) * C], bqk_raw[:, a], bias_mean[:, a:a + 1],
                                    None, ALU.subtract).then_inc(qk_bias_set, 1)

            def spread_bv():
                dve.wait_ge(qk_bias_set, 2)
                dve.wait_ge(small_in, 64)
                dve.wait_ge(constants_set, 4)
                for m in range(M):
                    V.tensor_scalar(bv_wide[:, m], ones[:], bv_col[:, m:m + 1], None,
                                    ALU.mult).then_inc(bv_spread, 1)

            def wvl_esel_lo():
                dve.wait_ge(wvl_hi, 1)
                V.tensor_tensor(wvl_l[:].rearrange("p m c -> p (m c)"), down_bank[0][:],
                                wvl_h[:].bitcast(F32).rearrange("p m c -> p (m c)"),
                                ALU.subtract).then_inc(wvl_lo, 1)
                dve.wait_ge(bvl_made, 1)
                V.tensor_copy(bvl[:], down_bank[1][:, 0:C]).then_inc(bvl_copied, 1)
                dve.wait_ge(bvl_copied, 1)
                V.tensor_tensor(out_bias[:], bvl[:], bln_raw, ALU.add).then_inc(out_bias_set, 1)
                dve.wait_ge(esel_hi, 1)
                V.tensor_tensor(esel_hl[:, :, LOW:LOW + E], esel_raw[:], esel_h[:, :, 0:E].bitcast(F32),
                                ALU.subtract).then_inc(esel_lo, 1)
                dve.wait_ge(out_bias_set, 1)

            def split_lo(it, s):
                sch = schedule(it)
                if s - 1 in sch["split_xT"] and has(it, 1):
                    h = sch["split_xT"][s - 1]
                    dve.wait_ge(xT_hi, half(it + 1, h))
                    V.tensor_tensor(xT_l[:, h], xT_raw[:], xT_h[:, h].bitcast(F32),
                                    ALU.subtract).then_inc(xT_lo, 1)
                if s - 1 in sch["split_x"] and has(it, 1):
                    i = sch["split_x"][s - 1]
                    pair_x = x_raw[:, 2 * i:2 * i + 2]
                    dve.wait_ge(x_hi, pair(it + 1, i))
                    V.tensor_tensor(x_l[:], pair_x, x_h[:].bitcast(F32), ALU.subtract).then_inc(x_lo, 1)
                if s in sch["bias_x"] and has(it, 1):
                    i = sch["bias_x"][s]
                    pair_x = x_raw[:, 2 * i:2 * i + 2]
                    dve.wait_ge(x_lo, pair(it + 1, i))
                    V.tensor_tensor(pair_x, pair_x, out_bias[:].unsqueeze(1).broadcast_to((P, 2, C)),
                                    ALU.add).then_inc(x_biased, 1)

            def layer_norm(dst, src, mv, rstd):
                return V.tensor_scalar(dst, src, mv[:, 0:1], rstd, ALU.subtract, ALU.mult)

            def early(it, s):
                for kind, a, off in transposed_first(
                        planned(it, s - 1, ("QK", "GG", "KS", "KV", "QT", "Y", "XT", "OT"))):
                    b = it + off
                    if kind == "QK":
                        dve.wait_ge(k_squared, tile(b, a))
                        V.tensor_scalar(k_sum_eps[:, a % 2:a % 2 + 1], k_sum[:, a % 2:a % 2 + 1], EPS_SUM,
                                        None, ALU.add).then_inc(k_eps, 1)
                        dve.wait_ge(k_eps, tile(b, a))
                        V.reciprocal(k_scale[:, a % 2:a % 2 + 1],
                                     k_sum_eps[:, a % 2:a % 2 + 1]).then_inc(k_scaled, 1)
                        if a == T - 1:
                            dve.wait_ge(q_fourth, tile(b, a))
                            V.tensor_scalar(q4_lifted[:], q4_sum[:], LIFT * LIFT, 1e-30, ALU.mult,
                                            ALU.max).then_inc(q_lifted, 1)
                            V.tensor_scalar(q_floor[:], q_sum[:], EPS_SUM, EPS_NORM * LIFT, ALU.add,
                                            ALU.mult).then_inc(q_floored, 1)
                    elif kind == "GG" and a == T - 1:
                        dve.wait_ge(g_hi, b + 1)
                        V.tensor_tensor(gT_l[:].rearrange("p m c -> p (m c)"), g_bank[:],
                                        gT_h[:].bitcast(F32).rearrange("p m c -> p (m c)"),
                                        ALU.subtract).then_inc(g_lo, 1)
                    elif kind == "KS":
                        dve.wait_ge(cols_rooted, b + 1)
                        V.reciprocal(col_scale[:], col_norm[:]).then_inc(cols_inverted, 1)
                        dve.wait_ge(cols_inverted, b + 1)
                        V.tensor_scalar(col_scale[:], col_scale[:], float(N) ** -0.5, None,
                                        ALU.mult).then_inc(cols_scaled, 1)
                    elif kind == "KV":
                        for m in range(M):
                            dve.wait_ge(kv_hi, b * M + m + 1)
                            V.scalar_tensor_tensor(out=kvw_l[:, m], in0=kvw[:, m], scalar=col_scale[:, m, 0:1],
                                                   in1=kvw_h[:, m].bitcast(F32), op0=ALU.mult,
                                                   op1=ALU.subtract).then_inc(kv_lo, 1)
                    elif kind == "QT":
                        dve.wait_ge(qT_hi, pair(b, a))
                        V.tensor_tensor(qT_l[:, a % 2].rearrange("p t m n -> p (t m n)"),
                                        ring_of(it, s - 1, kind, a)[:],
                                        qT_h[:, a % 2].bitcast(F32).rearrange("p t m n -> p (t m n)"),
                                        ALU.subtract).then_inc(qT_lo, 1)
                    elif kind == "Y":
                        dve.wait_ge(y_rooted, tile(b, a))
                        V.reciprocal(y_rstd[:, a % 2:a % 2 + 1], y_std[:, a % 2:a % 2 + 1]).then_inc(y_inverted, 1)
                        dve.wait_ge(y_inverted, tile(b, a))
                        at_least(dve, x1_transposed, tile(b - 1, a))
                        layer_norm(x1[:, a], y[:, a % 2], y_mv[:, a % 2],
                                   y_rstd[:, a % 2:a % 2 + 1]).then_inc(x1_made, 1)
                    elif kind == "XT":
                        g, i = divmod(a, GT)
                        dve.wait_ge(x1T_hi, tile(b, a))
                        V.tensor_tensor(x1T_l[:, g, :, i * P:(i + 1) * P],
                                        ring_of(it, s - 1, kind, a)[:, 0:C].rearrange("p (m n) -> p m n", m=M),
                                        x1T_h[:, g, :, i * P:(i + 1) * P].bitcast(F32),
                                        ALU.subtract).then_inc(x1T_lo, 1)
                    elif kind == "OT":
                        n = out_pair(it, off, a)
                        dve.wait_ge(z_rooted, n)
                        V.reciprocal(z_rstd[:, a], z_std[:, a]).then_inc(z_inverted, 1)
                        dve.wait_ge(z_inverted, n)
                        V.scalar_tensor_tensor(out=z_shift[:, a], in0=z_mv[:, a, :, 0], scalar=-1.0,
                                               in1=z_rstd[:, a], op0=ALU.mult, op1=ALU.mult
                                               ).then_inc(z_shift_made, 1)

            def late(it, s):
                for kind, a, off in planned(it, s, ("QK",)):
                    dve.wait_ge(qk_projected, tile(it + off, a))
                    at_least(dve, q_fourth, tile(it + off, a) - 1)
                    V.tensor_tensor(qk[:], qk_bank[:], qk_bias[:], ALU.add).then_inc(qk_biased, 1)
                for kind, a, off in planned(it, s - 1, ("QK",)):
                    n = tile(it + off, a)
                    p = a % 2
                    dve.wait_ge(k_hi, n)
                    V.scalar_tensor_tensor(out=k2_l[:, p], in0=k2[:, p], scalar=k_scale[:, p:p + 1],
                                           in1=k2_h[:, p].bitcast(F32), op0=ALU.mult,
                                           op1=ALU.subtract).then_inc(k_lo, 1)
                    if a == 0:
                        at_least(dve, cols_summed, it + off)
                        V.tensor_scalar(k2_total[:], k2[:, p], k_scale[:, p:p + 1], None,
                                        ALU.mult).then_inc(k_summed, 1)
                    else:
                        dve.wait_ge(k_summed, n - 1)
                        V.scalar_tensor_tensor(out=k2_total[:], in0=k2[:, p], scalar=k_scale[:, p:p + 1],
                                               in1=k2_total[:], op0=ALU.mult, op1=ALU.add).then_inc(k_summed, 1)
                    dve.wait_ge(k_fourth, n)
                    if a == 0:
                        V.tensor_copy(k4_total[:], k4[:]).then_inc(k4_summed, 1)
                    else:
                        dve.wait_ge(k4_summed, n - 1)
                        V.tensor_tensor(k4_total[:], k4_total[:], k4[:], ALU.add).then_inc(k4_summed, 1)
                    if a == T - 1:
                        b = it + off
                        dve.wait_ge(q_rooted, b + 1)
                        dve.wait_ge(q_floored, b + 1)
                        V.tensor_tensor(q_root[:], q_root[:], q_floor[:], ALU.max).then_inc(q_max, 1)
                        dve.wait_ge(q_max, b + 1)
                        V.reciprocal(q_scale[:], q_root[:]).then_inc(q_scale_set, 1)
                for kind, a, off in planned(it, s, ("KS", "KV", "Y", "LG", "OT")):
                    b = it + off
                    if kind == "KS":
                        dve.wait_ge(cols_summed, b + 1)
                        sums = ring_of(it, s, kind, a)
                        V.tensor_scalar(col_sums[:, 0:M].rearrange("p a b -> p (a b)"), sums[:, 0:2 * M],
                                        EPS_NORM ** 2, None, ALU.max)
                        V.tensor_copy(col_sums[:, M:2 * M].rearrange("p a b -> p (a b)"),
                                      sums[:, 2 * M:4 * M]).then_inc(cols_copied, 1)
                    elif kind == "KV":
                        dve.wait_ge(kv_projected, b + 1)
                        dve.wait_ge(cols_copied, b + 1)
                        for m in range(M):
                            V.scalar_tensor_tensor(out=kvw[:, m], in0=bvl[:], scalar=col_sums[:, M + m, 0:1],
                                                   in1=ring_of(it, s, kind, a)[:, m * C:(m + 1) * C],
                                                   op0=ALU.mult, op1=ALU.add).then_inc(kv_summed, 1)
                    elif kind == "LG":
                        dve.wait_ge(logits_low, half(b, a))
                        V.tensor_tensor(sel[:], ring_of(it, s, kind, a)[0:E, :], sel[:],
                                        ALU.add).then_inc(logits_summed, 1)
                    elif kind == "Y":
                        n = tile(b, a)
                        dve.wait_ge(y_projected, n)
                        dve.wait_ge(x_biased, pair(b, a // 2))
                        V.tensor_tensor(y[:, a % 2], ring_of(it, s, kind, a)[:, 0:C], x_raw[:, a],
                                        ALU.add).then_inc(y_added, 1)
                        dve.wait_ge(y_added, n)
                        V.bn_stats(y_stats[:, a % 2], y[:, a % 2]).then_inc(y_stated, 1)
                        stand_at(dve, y_stated, n)
                        V.bn_aggr(y_mv[:, a % 2], y_stats[:, a % 2]).then_inc(y_aggregated, 1)
                    elif kind == "OT":
                        n = out_pair(it, off, a)
                        t = GT * (off % G) + 2 * a
                        dve.wait_ge(o_transposed, n)
                        at_least(dve, stored[a], it * (16 * G) + off * 16)
                        if isinstance(it, int) and it == 0:
                            dve.wait_ge(piece_lo, WPIECES)
                        V.tensor_tensor(z[:, a].rearrange("p t c -> p (t c)"), ring_of(it, s, kind, a)[:],
                                        x1[:, t:t + 2].rearrange("p t c -> p (t c)"),
                                        ALU.add).then_inc(z_added, 1)
                        dve.wait_ge(z_added, n)
                        for i in range(2):
                            V.bn_stats(z_stats[:, a, i], z[:, a, i]).then_inc(z_stated, 1)
                        for i in range(2):
                            stand_at(dve, z_stated, 2 * n - 1 + i)
                            V.bn_aggr(z_mv[:, a, i], z_stats[:, a, i]).then_inc(z_aggregated, 1)
                if s in schedule(it)["scale_q"] and has(it, 1):
                    for t in schedule(it)["scale_q"][s]:
                        dve.wait_ge(q_scale_set, it + 2)
                        V.tensor_scalar(q2[:, t], q2[:, t], q_scale[:, t:t + 1], LIFT, ALU.mult,
                                        ALU.mult).then_inc(q_scaled, 1)

            def step(it, s):
                early(it, s)
                split_lo(it, s)
                if it_is(it, s, 5):
                    wqk_split_lo()
                if it_is(it, s, 6):
                    spread_bv()
                if it_is(it, s, 10):
                    wvl_esel_lo()
                if step_exists(it, s):
                    f = step_no(it, s)
                    dve.wait_ge(up_made, f + 1)
                    dve.wait_ge(sel_spread, f + 1)
                    at_least(dve, gated_lo, f)
                    V.scalar_tensor_tensor(out=gated[:], in0=up_bank[s % 2][:], scalar=0.0,
                                           in1=sel_all[:, s % 2], op0=ALU.max,
                                           op1=ALU.mult).then_inc(gate_applied, 1)
                late(it, s)
                if step_exists(it, s):
                    dve.wait_ge(gated_hi, f + 1)
                    V.tensor_tensor(gated_l[:, s % 2], gated[:],
                                    gated_h[:, s % 2].bitcast(F32), ALU.subtract).then_inc(gated_lo, 1)

            run(dve, step)

        @block.tensor
        def _(pe):
            mm = nc.tensor.matmul

            def product(dst, pairs, start, stop=True, **kw):
                n = 3 * len(pairs)
                i = 0
                for (lh, ll), (rh, rl) in pairs:
                    for lhs, rhs in ((lh, rh), (lh, rl), (ll, rh)):
                        last = mm(dst, lhs, rhs, start=start and i == 0, stop=stop and i == n - 1, **kw)
                        i += 1
                return last

            def both(hi, lo, *index):
                return hi[index], lo[index]

            def make_wvl():
                pe.wait_ge(w_v_in, 16)
                pe.wait_ge(w_ln_in, 16)
                for c in range(M):
                    for m in range(M):
                        last = mm(down_bank[0][:, c * C:(c + 1) * C], wvT_raw[:, m, c * P:(c + 1) * P],
                                  wln_raw[:, m], start=(m == 0), stop=(m == M - 1))
                last.then_inc(wvl_made, 1)
                pe.wait_ge(bv_spread, M)
                for m in range(M):
                    last = mm(down_bank[1][:, 0:C], bv_wide[:, m], wln_raw[:, m], start=(m == 0),
                              stop=(m == M - 1))
                last.then_inc(bvl_made, 1)

            pe.wait_ge(wqk_lo, 2 * M)

            ALL = slice(None)

            def layer1(it, s):
                for kind, a, off in planned(it, s, ("QK", "GG", "KS", "KV", "QT", "Y", "XT", "LG", "OT")):
                    b = it + off
                    if kind in RING_KINDS:
                        bk, read, count = ring_place(it, s, kind, a)
                        if read is not None:
                            at_least(pe, read, count)
                    if kind == "QK":
                        h, i = divmod(a, GT)
                        pe.wait_ge(xT_lo, half(b, h))
                        at_least(pe, qk_biased, tile(b, a) - 1)
                        product(qk_bank[:], [(both(xT_h, xT_l, ALL, h, m, slice(i * P, (i + 1) * P)),
                                              both(wqk_h, wqk_l, ALL, m, ALL)) for m in range(M)],
                                start=True).then_inc(qk_projected, 1)
                    elif kind == "GG":
                        pe.wait_ge(k_lo, tile(b, a))
                        pe.wait_ge(x_lo, pair(b, a // 2))
                        if a == 0:
                            at_least(pe, g_lo, b)
                        for m in range(M):
                            last = product(g_bank[:, m * C:(m + 1) * C],
                                           [(both(x_h, x_l, ALL, a % 2, slice(m * P, (m + 1) * P)),
                                             both(k2_h, k2_l, ALL, a % 2, ALL))],
                                           start=(a == 0 and m == 0), stop=(a == T - 1),
                                           skip_group_check=True)
                        last.then_inc(g_added, 1)
                    elif kind == "KS":
                        pe.wait_ge(k_summed, tile(b, T - 1))
                        pe.wait_ge(k4_summed, tile(b, T - 1))
                        for i, total in enumerate((k4_total, k2_total)):
                            for m in range(M):
                                j = 2 * (i * M + m)
                                last = mm(bk[:, j:j + 2], total[:, m * P:(m + 1) * P], ones[:, 0:2],
                                          start=True, stop=True)
                        last.then_inc(cols_summed, 1)
                    elif kind == "KV":
                        pe.wait_ge(g_lo, b + 1)
                        for c in range(M):
                            last = product(bk[:, c * C:(c + 1) * C],
                                           [(both(gT_h, gT_l, ALL, m, slice(c * P, (c + 1) * P)),
                                             both(wvl_h, wvl_l, ALL, m, ALL)) for m in range(M)], start=True)
                        last.then_inc(kv_projected, 1)
                    elif kind == "QT":
                        pe.wait_ge(q_scaled, tile(b, 2 * a + 1))
                        for i in range(2):
                            for m in range(M):
                                j = (i * M + m) * P
                                last = nc.tensor.transpose(bk[:, j:j + P], q2[:, 2 * a + i, m * P:(m + 1) * P],
                                                           ident[:])
                        last.then_inc(q_transposed, 1)
                    elif kind == "Y":
                        h, i = divmod(a, GT)
                        pe.wait_ge(qT_lo, pair(b, a // 2))
                        pe.wait_ge(kv_lo, b * M + M)
                        product(bk[:, 0:C],
                                [(both(xT_h, xT_l, ALL, h, m, slice(i * P, (i + 1) * P)),
                                  both(wvl_h, wvl_l, ALL, m, ALL)) for m in range(M)] +
                                [(both(qT_h, qT_l, ALL, (a // 2) % 2, a % 2, m, ALL),
                                  both(kvw_h, kvw_l, ALL, m, ALL)) for m in range(M)],
                                start=True).then_inc(y_projected, 1)
                    elif kind == "XT":
                        pe.wait_ge(x1_made, tile(b, a))
                        for m in range(M):
                            last = nc.tensor.transpose(bk[:, m * P:(m + 1) * P], x1[:, a, m * P:(m + 1) * P],
                                                       ident[:])
                        last.then_inc(x1_transposed, 1)
                    elif kind == "LG":
                        pe.wait_ge(x1T_lo, tile(b, GT * a + GT - 1))
                        for m in range(M):
                            mm(bk[:], esel_hl[:, m], x1T_h[:, a, m], start=(m == 0), stop=False)
                            last = mm(bk[:], esel_h[:, m], x1T_l[:, a, m], start=False, stop=(m == M - 1))
                        last.then_inc(logits_made, 1)
                    elif kind == "OT":
                        n = out_pair(it, off, a)
                        pe.wait_ge(o_copied, n - a - 1 + M)
                        for i in range(2):
                            for m in range(M):
                                j = (i * M + m) * P
                                t = 2 * a + i
                                last = nc.tensor.transpose(bk[:, j:j + P], oT[:, m, t * P:(t + 1) * P], ident[:])
                        last.then_inc(o_transposed, 1)

            def step(it, s):
                if step_exists(it, s):
                    g, e = divmod(s, E)
                    f = step_no(it, s)
                    if e == 0:
                        pe.wait_ge(x1T_lo, tile(it, GT * g + GT - 1))
                    if first_group(it, g) and e % (E // 4) == 0:
                        pe.wait_ge(piece_lo, 2 * (e // 4) + 1)
                    at_least(pe, gate_applied, f - 1)
                    product(up_bank[s % 2][:], [(both(keys_h, keys_l, ALL, e, m, ALL),
                                                 both(x1T_h, x1T_l, ALL, g, m, ALL)) for m in range(M)],
                            start=True).then_inc(up_made, 1)
                layer1(it, s)
                if it_is(it, s, 8):
                    make_wvl()
                if it_is(it, s, 15):
                    pe.wait_ge(wvl_lo, 1)
                    pe.wait_ge(esel_lo, 1)
                    pe.wait_ge(out_bias_set, 1)
                if step_exists(it, s, LAG):
                    e = (s - LAG) % E
                    f = step_no(it, s, LAG)
                    grp = 2 * it + (s - LAG) // E
                    pe.wait_ge(gated_lo, f + 1)
                    if first_group(it, (s - LAG) // E) and e % (E // 4) == 0:
                        pe.wait_ge(piece_lo, 2 * (e // 4) + 2)
                    if e == 0:
                        at_least(pe, o_copied, M * grp)
                    for c in range(M):
                        r = (s - LAG) % 2
                        last = product(down_bank[c][:], [(both(vals_h, vals_l, ALL, e, slice(c * P, (c + 1) * P)),
                                                          both(gated_h, gated_l, ALL, r, ALL))],
                                       start=(e == 0), stop=(e == E - 1))
                    last.then_inc(down_made, 1)

            run(pe, step)


def kernel(**inputs):
    import numpy as np
    import concourse.bacc as bacc
    from concourse.bass_utils import run_bass_kernel_spmd

    def given(name):
        return np.asarray(inputs["L0_" + name])

    def chunked(w):
        return w.reshape(-1, P, w.shape[-1]).transpose(1, 0, 2)

    x = given("attn_x")
    w = given("attn_Wqkv")
    b = given("attn_bqkv")
    arrays = {
        "x": x,
        "xT": x.reshape(B, P, G, GT, M, P).transpose(0, 5, 2, 4, 3, 1).reshape(B, P, G, M, GN),
        "wqk": chunked(w[:, 0:2 * C]).reshape(P, M, 2, C),
        "wvT": chunked(w[:, 2 * C:].T),
        "wln": chunked(given("attn_Wln")),
        "b_qk": b[0:2 * C].reshape(2, C),
        "b_v": b[2 * C:].reshape(M, P).T,
        "b_ln": given("attn_bln"),
        "esel": chunked(given("ffn_expert_sel").T),
        "keys": given("ffn_keys").reshape(E, M, P, H).transpose(2, 0, 1, 3).reshape(P, E * M * H),
        "values": given("ffn_values").transpose(1, 0, 2).reshape(P, E * C),
        "ident": np.eye(P, dtype=np.float32),
    }
    arrays = {name: np.ascontiguousarray(a) for name, a in arrays.items()}
    nc = bacc.Bacc("TRN2", target_bir_lowering=False, num_devices=1)
    aps = [nc.dram_tensor("in_" + name, a.shape, mybir.dt.from_np(a.dtype), kind="ExternalInput").ap()
           for name, a in arrays.items()]
    out = nc.dram_tensor("out", (B, N, C), F32, kind="ExternalOutput").ap()
    build_program(nc, *aps, out)
    r = run_bass_kernel_spmd(nc, [{"in_" + name: a for name, a in arrays.items()}], core_ids=[0])
    return r.results[0]["out"]
```

```python
from contextlib import ExitStack

import concourse.bass as bass
from concourse import mybir

F32 = mybir.dt.float32
F32R = mybir.dt.float32r
ALU = mybir.AluOpType
ACT = mybir.ActivationFunctionType
AX_X = mybir.AxisListType.X

P = 128
B, N, C = 8, 1024, 256
E, H = 16, 128
M = C // P
T = N // P
GT = 4
GN = GT * P
G = T // GT
STEPS = G * E
LAG = 1
LOW = 32
EPS_SUM = 1e-7
EPS_NORM = 1e-12
EPS_LN = 1e-5
LIFT = 2.0 ** 20
WPIECES = 8
WPIECE = 2 * M * E * H // WPIECES

LOOP = dict(
    plan={
        0: [("QT", 2)], 1: [("QT", 3)], 2: [("OT", 0), ("Y", 4)], 3: [("OT", 1)], 4: [("Y", 5)],
        5: [("Y", 6), ("XT", 4)], 6: [("Y", 7), ("XT", 5)], 7: [("XT", 6), ("QK", 0)],
        8: [("XT", 7), ("QK", 1)], 9: [("GG", 0)], 10: [("QK", 2), ("GG", 1), ("LG", 1)], 11: [("QK", 3)],
        12: [("GG", 2), ("QK", 4)], 13: [("GG", 3)], 14: [("QK", 5)], 15: [("GG", 4), ("QK", 6)],
        16: [("GG", 5)], 17: [("QK", 7)], 18: [("GG", 6)], 19: [("KS", 0), ("OT", 0), ("GG", 7)],
        20: [("OT", 1)], 21: [("KV", 0), ("QT", 0)], 22: [("QT", 1)], 23: [("Y", 0)],
        24: [("Y", 1), ("XT", 0)], 25: [("Y", 2), ("XT", 1)], 26: [("Y", 3)], 27: [("XT", 2), ("XT", 3)],
        29: [("LG", 0)],
    },
    split_xT={4: 0, 9: 1}, split_x={5: 0, 10: 1, 13: 2, 16: 3},
    bias_x={9: 0, 14: 1, 28: 2, 30: 3},
    scale_q={19: (0, 1), 21: (2, 3), 30: (4, 5), 31: (6, 7)},
    gpsimd_xT=(), gpsimd_x=())
FIRST = dict(
    plan={
        7: [("QK", 0)], 8: [("QK", 1)], 9: [("QK", 2), ("GG", 0)], 10: [("QK", 3), ("GG", 1)],
        11: [("QK", 4), ("GG", 2)], 12: [("QK", 5), ("GG", 3)], 13: [("QK", 6), ("GG", 4)],
        14: [("QK", 7), ("GG", 5)], 15: [("GG", 6), ("GG", 7)], 16: [("KS", 0)],
        17: [("QT", 0), ("KV", 0), ("QT", 1)], 18: [("Y", 0), ("Y", 1)],
        19: [("Y", 2), ("Y", 3), ("XT", 0), ("XT", 1)], 20: [("XT", 2), ("XT", 3)], 21: [("LG", 0)],
    },
    split_xT={4: 0, 8: 1}, split_x={5: 0, 8: 1, 10: 2, 13: 3},
    bias_x={17: 0, 18: 1, 20: 2, 21: 3},
    scale_q={15: (0, 1, 2), 16: (3,), 24: (4, 5, 6, 7)},
    gpsimd_xT=(1,), gpsimd_x=())
LAST = dict(plan={1: [("OT", 0), ("OT", 1)]}, split_xT={}, split_x={}, bias_x={}, scale_q={},
            gpsimd_xT=(), gpsimd_x=())
LAST_STEPS = 3
RING_KINDS = ("QT", "Y", "XT", "LG", "OT", "KS", "KV")
FIRST_STEP = min(FIRST["split_xT"])
SETUP_STEPS = (5, 8, 9, 10)
SIGMOID_STEP = 20
PIECE_STEPS = ((-1, 9), (-1, 17), (-1, 18), (-1, 20), (0, 1), (0, 3), (0, 5), (0, 7))
PIECE_LOADS = ((-1, 16), (-1, 17), (-1, 24), (-1, 25), (0, 1), (0, 3))


def batch_offset(kind, a):
    if kind in ("Y", "XT"):
        return int(a < GT)
    if kind == "QT":
        return int(a < T // 4)
    if kind == "LG":
        return 1 - a
    return 1


def schedule(it):
    if isinstance(it, int) and (it < 0 or it == B):
        return FIRST if it < 0 else LAST
    return LOOP


def stages(it, s):
    out = []
    for kind, a in schedule(it)["plan"].get(s, ()):
        if kind == "OT":
            g = 0 if s >= E else -1
            if 0 <= G * it + g < G * B:
                out.append((kind, a, g))
        elif 0 <= it + batch_offset(kind, a) < B:
            out.append((kind, a, batch_offset(kind, a)))
    return out


def ring_uses():
    return [(it, s, kind, a, off) for it in range(-1, B + 1) for s in range(STEPS)
            if not (it < 0 and s < FIRST_STEP) for kind, a, off in stages(it, s) if kind in RING_KINDS]


RING = ring_uses()
RING_AT = {u[:4]: n for n, u in enumerate(RING)}


def build_program(nc, x, xT, wqk, wvT, wln, b_qk, b_v, b_ln, esel, keys, values, ident_in, out):
    with ExitStack() as ctx:
        def sb(name, shape, dt=F32):
            return ctx.enter_context(nc.sbuf_tensor(name, shape, dt))

        def bank(name):
            return ctx.enter_context(nc.psum_tensor(name, [P, 512], F32))

        def sem(name):
            return ctx.enter_context(nc.semaphore(name))

        keys_h, keys_l = sb("keys_h", [P, E, M, H], F32R), sb("keys_l", [P, E, M, H], F32R)
        vals_h, vals_l = sb("vals_h", [P, E, C], F32R), sb("vals_l", [P, E, C], F32R)
        wqk_h, wqk_l = sb("wqk_h", [P, M, 2 * C], F32R), sb("wqk_l", [P, M, 2 * C], F32R)
        wvl_h, wvl_l = sb("wvl_h", [P, M, C], F32R), sb("wvl_l", [P, M, C], F32R)
        esel_h, esel_hl = sb("esel_h", [P, M, P], F32R), sb("esel_hl", [P, M, P], F32R)
        qk_bias = sb("qk_bias", [P, 2 * C])
        bvl = sb("bvl", [P, C])
        out_bias = sb("out_bias", [P, C])
        ident = sb("ident", [P, P])
        ones = sb("ones", [P, P])
        eps_ln = sb("eps_ln", [P, 1])

        x_raw = sb("x_raw", [P, T, C])
        xT_raw = sb("xT_raw", [P, M, GN])
        xT_h, xT_l = sb("xT_h", [P, G, M, GN], F32R), sb("xT_l", [P, G, M, GN], F32R)
        x_h, x_l = sb("x_h", [P, 2, C], F32R), sb("x_l", [P, 2, C], F32R)
        qk = sb("qk", [P, 2 * C])
        q2 = sb("q2", [P, T, C])
        q_sum, q4_sum, q_root, q_floor, q_scale = (sb(n, [P, T]) for n in (
            "q_sum", "q4_sum", "q_root", "q_floor", "q_scale"))
        q4_lifted = sb("q4_lifted", [P, T])
        k2, k4 = sb("k2", [P, 2, C]), sb("k4", [P, C])
        k_sum, k_sum_eps, k_scale = (sb(n, [P, 2]) for n in ("k_sum", "k_sum_eps", "k_scale"))
        k2_h, k2_l = sb("k2_h", [P, 2, C], F32R), sb("k2_l", [P, 2, C], F32R)
        k2_total, k4_total = sb("k2_total", [P, C]), sb("k4_total", [P, C])
        col_sums = sb("col_sums", [P, 4, 2])
        col_norm, col_scale = sb("col_norm", [P, M, 2]), sb("col_scale", [P, M, 2])
        gT_h, gT_l = k2_h, k2_l
        kvw_h, kvw_l = sb("kvw_h", [P, M, C], F32R), sb("kvw_l", [P, M, C], F32R)
        qT_h, qT_l = sb("qT_h", [P, 2, 2, M, P], F32R), sb("qT_l", [P, 2, 2, M, P], F32R)
        y = sb("y", [P, 2, C])
        y_stats, y_mv = sb("y_stats", [P, 2, 6]), sb("y_mv", [P, 2, 2])
        y_std, y_rstd = sb("y_std", [P, 2]), sb("y_rstd", [P, 2])
        kvw = y
        x1 = sb("x1", [P, T, C])
        x1T_h, x1T_l = sb("x1T_h", [P, G, M, GN], F32R), sb("x1T_l", [P, G, M, GN], F32R)

        sel = sb("sel", [E, GN])
        sel_rows = sb("sel_rows", [P, E // 4, GN])
        sel_all = sb("sel_all", [P, 2, GN])
        gated = sb("gated", [P, GN])
        gated_h, gated_l = sb("gated_h", [P, 2, GN], F32R), sb("gated_l", [P, 2, GN], F32R)
        oT = sb("oT", [P, M, GN])
        z = sb("z", [P, 2, 2, C])
        z_stats, z_mv = sb("z_stats", [P, 2, 2, 6]), sb("z_mv", [P, 2, 2, 2])
        z_std, z_rstd, z_shift = (sb(n, [P, 2, 2]) for n in ("z_std", "z_rstd", "z_shift"))

        w_stage = [oT[:].rearrange("p a n -> p (a n)"), z[:].rearrange("p a t c -> p (a t c)")]
        wqk_raw = x1[:, 0:4, :].rearrange("p (m a) c -> p m a c", m=M)
        wvT_raw, wln_raw = x1[:, 4:6, :], x1[:, 6:8, :]
        wqk_flat = wqk_raw.rearrange("p m a c -> p (m a) c")
        wqk_hi_flat = wqk_h[:].rearrange("p m (a c) -> p (m a) c", a=2)
        wqk_lo_flat = wqk_l[:].rearrange("p m (a c) -> p (m a) c", a=2)
        minus_mean, bias_mean = sb("minus_mean", [P, 2 * M]), sb("bias_mean", [P, 2])
        bqk_raw = sel_all[:, 0].rearrange("p (a c) -> p a c", a=2)
        bln_raw = y[:, 1]
        bv_col = sb("bv_col", [P, M])
        bv_wide = y[:, 0].rearrange("p (m n) -> p m n", m=M)
        table_ahead = sb("table_ahead", [P, 2])
        esel_raw = sb("esel_raw", [P, M, E])

        up_bank = [bank("up_bank0"), bank("up_bank1")]
        down_bank = [bank("down_bank0"), bank("down_bank1")]
        qk_bank, g_bank = bank("qk_bank"), bank("g_bank")
        ring_bank = [bank("ring_bank0"), bank("ring_bank1")]

        (w_qk_in, w_v_in, w_ln_in, bias_in, small_in) = map(sem, (
            "w_qk_in", "w_v_in", "w_ln_in", "bias_in", "small_in"))
        piece_in = [sem("piece_in0"), sem("piece_in1")]
        piece_hi, piece_lo = sem("piece_hi"), sem("piece_lo")
        (constants_set, wqk_summed, wqk_mean_set, wqk_hi, wqk_lo, bias_summed, bias_mean_set, qk_bias_set,
         bv_spread, wvl_made, wvl_hi, wvl_lo, esel_hi, esel_lo, bvl_made, bvl_copied, out_bias_set) = map(sem, (
             "constants_set", "wqk_summed", "wqk_mean_set", "wqk_hi", "wqk_lo", "bias_summed",
             "bias_mean_set", "qk_bias_set", "bv_spread", "wvl_made", "wvl_hi", "wvl_lo", "esel_hi",
             "esel_lo", "bvl_made", "bvl_copied", "out_bias_set"))
        x_in, xT_in = [sem("x_in0"), sem("x_in1")], sem("xT_in")
        xT_hi, xT_lo = sem("xT_hi"), sem("xT_lo")
        x_hi, x_lo, x_biased = map(sem, ("x_hi", "x_lo", "x_biased"))
        (qk_projected, qk_biased, q_squared, k_squared, q_fourth, k_eps, k_scaled, k_hi, k_fourth, k_lo,
         k_summed, k4_summed, g_added) = map(sem, (
             "qk_projected", "qk_biased", "q_squared", "k_squared", "q_fourth", "k_eps", "k_scaled",
             "k_hi", "k_fourth", "k_lo", "k_summed", "k4_summed", "g_added"))
        (q_lifted, q_rooted, q_floored, q_max, q_scale_set, g_hi, g_lo, cols_summed, cols_copied,
         cols_rooted, cols_inverted, kv_projected, cols_scaled) = map(sem, (
             "q_lifted", "q_rooted", "q_floored", "q_max", "q_scale_set", "g_hi", "g_lo", "cols_summed",
             "cols_copied", "cols_rooted", "cols_inverted", "kv_projected", "cols_scaled"))
        kv_summed, kv_hi, kv_lo = map(sem, ("kv_summed", "kv_hi", "kv_lo"))
        q_scaled = sem("q_scaled")
        q_transposed, qT_hi, qT_lo = map(sem, ("q_transposed", "qT_hi", "qT_lo"))
        (y_projected, y_added, y_stated, y_aggregated, y_rooted, y_inverted, x1_made, x1_transposed,
         x1T_hi, x1T_lo) = map(sem, (
             "y_projected", "y_added", "y_stated", "y_aggregated", "y_rooted", "y_inverted", "x1_made",
             "x1_transposed", "x1T_hi", "x1T_lo"))
        logits_made, logits_low, logits_summed, sel_made = map(sem, (
            "logits_made", "logits_low", "logits_summed", "sel_made"))
        rows_in = [sem("rows_in%d" % j) for j in range(4)]
        sel_spread, up_made, gate_applied, gated_hi, gated_lo, down_made = map(sem, (
            "sel_spread", "up_made", "gate_applied", "gated_hi", "gated_lo", "down_made"))
        last_out_made = sem("last_out_made")
        last_half_made = sem("last_half_made")
        o_copied = sem("o_copied")
        (o_transposed, z_added, z_stated, z_aggregated, z_rooted, z_inverted, z_shift_made, out_made) = map(sem, (
            "o_transposed", "z_added", "z_stated", "z_aggregated", "z_rooted", "z_inverted",
            "z_shift_made", "out_made"))
        stored = [sem("stored0"), sem("stored1")]
        stood = sem("stood")

        def tile(b, t):
            return b * T + (t + 1)

        def pair(b, p):
            return b * (T // 2) + (p + 1)

        def half(b, h):
            return b * G + (h + 1)

        def out_pair(it, goff, p):
            return it * (2 * G) + (goff * 2 + p + 1)

        def at_least(eng, sm, count):
            if not isinstance(count, int) or count > 0:
                eng.wait_ge(sm, count)

        def stand_at(eng, sm, count):
            at_least(eng, sm, count)
            if not isinstance(count, int):
                eng.sem_inc(stood, 1)

        def ring_place(it, s, kind, a):
            rep = it if isinstance(it, int) else 1
            n = RING_AT[(rep, s, kind, a)]
            if n < 2:
                return ring_bank[n % 2], None, 0
            pit, ps, pkind, pa, poff = RING[n - 2]
            b = it + (pit - rep) + poff
            if pkind == "OT":
                return ring_bank[n % 2], z_added, out_pair(it + (pit - rep), poff, pa)
            read = {"QT": lambda: (qT_lo, pair(b, pa)), "Y": lambda: (y_added, tile(b, pa)),
                    "XT": lambda: (x1T_lo, tile(b, pa)), "LG": lambda: (logits_summed, half(b, pa)),
                    "KS": lambda: (cols_copied, b + 1), "KV": lambda: (kv_summed, b * M + M)}[pkind]()
            return (ring_bank[n % 2],) + read

        def ring_of(it, s, kind, a):
            rep = it if isinstance(it, int) else 1
            return ring_bank[RING_AT[(rep, s, kind, a)] % 2]

        def planned(it, s, kinds):
            return [(k, a, off) for k, a, off in stages(it if isinstance(it, int) else 1, s) if k in kinds]

        def transposed_first(planned_stages):
            return sorted(planned_stages, key=lambda stage: stage[0] != "XT")

        def has(it, off, lo=0):
            return not isinstance(it, int) or lo <= it + off < B

        def run(eng, step):
            for s in range(FIRST_STEP, STEPS):
                step(-1, s)
            for s in range(STEPS):
                step(0, s)
            with eng.Fori(1, B - 1) as it:
                for s in range(STEPS):
                    step(it, s)
            for s in range(STEPS):
                step(B - 1, s)
            for s in range(LAST_STEPS):
                step(B, s)

        def it_is(it, s, first):
            return isinstance(it, int) and it < 0 and s == first

        def first_iteration(it):
            return isinstance(it, int) and it < 0

        def qk_bank_of(it, t):
            return up_bank[1] if first_iteration(it) and t % 2 else qk_bank

        def qk_of(it, t):
            return gated if first_iteration(it) and t % 2 else qk

        def x_h_of(it, i):
            return gated_h[:, :, 0:C] if first_iteration(it) and i % 2 else x_h[:]

        def x_l_of(it, i):
            return gated_l[:, :, 0:C] if first_iteration(it) and i % 2 else x_l[:]

        def last_iteration(it):
            return isinstance(it, int) and it == B

        def step_exists(it, s, lag=0):
            return not isinstance(it, int) or 0 <= it * STEPS + s - lag < B * STEPS

        def step_no(it, s, lag=0):
            return it * STEPS + (s - lag)

        x_dram = x.rearrange("b (p t) c -> b p t c", t=T)
        out_dram = out.rearrange("b (p t) c -> b p t c", t=T)
        keys_flat = [keys_h[:].rearrange("p e m h -> p (e m h)"), keys_l[:].rearrange("p e m h -> p (e m h)")]
        vals_flat = [vals_h[:].rearrange("p e c -> p (e c)"), vals_l[:].rearrange("p e c -> p (e c)")]

        def piece(i, part):
            flat = (keys_flat, vals_flat)[i % 2]
            return flat[part][:, (i // 2) * WPIECE:(i // 2 + 1) * WPIECE]

        def first_group(it, g):
            return isinstance(it, int) and it == 0 and g == 0

        block = ctx.enter_context(nc.Block())

        @block.sync
        def _(sp):
            def load_half(it, h):
                at_least(sp, xT_lo, half(it + 1, h) - 1)
                sp.dma_start(xT_raw[:], xT[it + 1, :, h]).then_inc(xT_in, 16)
                at_least(sp, y_added, tile(it, GT * h + GT - 1))
                sp.dma_start(x_raw[:, GT * h:GT * h + GT],
                             x_dram[it + 1, :, GT * h:GT * h + GT]).then_inc(x_in[h], 16)

            def load_piece(i):
                src = (keys, values)[i % 2]
                sp.dma_start(w_stage[i % 2], src[:, (i // 2) * WPIECE:(i // 2 + 1) * WPIECE]
                             ).then_inc(piece_in[i % 2], 16)

            def store_pair(it, goff, p):
                if last_iteration(it):
                    sp.wait_ge(out_made, 2 * out_pair(it, goff, -1) + p + 1)
                    sp.wait_ge(last_out_made, p + 1)
                else:
                    at_least(sp, out_made, 2 * out_pair(it, goff, p))
                g = goff % G
                b = it + (goff - g) // G
                t = GT * g + 2 * p
                sp.dma_start(out_dram[b, :, t:t + 2], z[:, p]).then_inc(stored[p], 16)

            def move_rows(it, off, g):
                stand_at(sp, sel_made, half(it + off, g))
                at_least(sp, sel_spread, (it + off) * STEPS + g * E)
                for j in (1, 2, 3, 0):
                    sp.dma_start(sel_rows[0:P:32, j], sel[j:E:4, :]).then_inc(rows_in[j], 16)

            sp.dma_start(wqk_raw, wqk).then_inc(w_qk_in, 16)
            sp.dma_start(xT_raw[:], xT[0, :, 0]).then_inc(xT_in, 16)
            sp.dma_start(bqk_raw, b_qk.partition_broadcast(P)).then_inc(bias_in, 16)
            sp.dma_start(x_raw[:, 0:GT], x_dram[0, :, 0:GT]).then_inc(x_in[0], 16)
            sp.dma_start(wvT_raw, wvT).then_inc(w_v_in, 16)
            sp.dma_start(wln_raw, wln).then_inc(w_ln_in, 16)
            for dst, src in ((bln_raw, b_ln.partition_broadcast(P)), (bv_col[:], b_v), (esel_raw[:], esel),
                             (ident[:], ident_in)):
                sp.dma_start(dst, src).then_inc(small_in, 16)
            load_half(-1, 1)
            for i in range(2):
                load_piece(i)

            def step(it, s):
                if isinstance(it, int) and (it, s) in PIECE_LOADS:
                    i = 2 + PIECE_LOADS.index((it, s))
                    sp.wait_ge(piece_lo, i - 1)
                    load_piece(i)
                if s == 0 and has(it, 1):
                    load_half(it, 0)
                if s == 7 and has(it, 1) and not (isinstance(it, int) and it < 0):
                    load_half(it, 1)
                for kind, a, off in planned(it, s, ("LG", "OT")):
                    if kind == "LG":
                        move_rows(it, off, a)
                    else:
                        store_pair(it, off, a)

            run(sp, step)
            for p in range(2):
                sp.wait_ge(stored[p], 16 * G * B)

        @block.gpsimd
        def _(pool):
            nc.gpsimd.memset(ones[:], 1.0).then_inc(constants_set, 1)
            nc.gpsimd.memset(eps_ln[:], EPS_LN).then_inc(constants_set, 1)
            nc.gpsimd.memset(esel_h[:].bitcast(F32), 0.0).then_inc(constants_set, 1)
            nc.gpsimd.memset(esel_hl[:].bitcast(F32), 0.0).then_inc(constants_set, 1)

            def weights_lo(i):
                pool.wait_ge(piece_hi, i + 1)
                nc.gpsimd.tensor_tensor(piece(i, 1), w_stage[i % 2], piece(i, 0).bitcast(F32),
                                        ALU.subtract).then_inc(piece_lo, 1)

            for s in range(FIRST_STEP, STEPS):
                if FIRST["split_x"].get(s - 1) in FIRST["gpsimd_x"]:
                    i = FIRST["split_x"][s - 1]
                    pool.wait_ge(x_hi, i + 1)
                    nc.gpsimd.tensor_tensor(x_l_of(-1, i), x_raw[:, 2 * i:2 * i + 2], x_h_of(-1, i).bitcast(F32),
                                            ALU.subtract).then_inc(x_lo, 1)
                if FIRST["split_xT"].get(s - 1) in FIRST["gpsimd_xT"]:
                    h = FIRST["split_xT"][s - 1]
                    pool.wait_ge(xT_hi, h + 1)
                    nc.gpsimd.tensor_tensor(xT_l[:, h], xT_raw[:], xT_h[:, h].bitcast(F32),
                                            ALU.subtract).then_inc(xT_lo, 1)
                for kind, t, off in planned(-1, s - 1, ("QK",)):
                    if t > 0:
                        pool.wait_ge(k_fourth, tile(0, t))
                        pool.wait_ge(k4_summed, tile(0, t - 1))
                        nc.gpsimd.tensor_tensor(k4_total[:], k4_total[:], k4[:], ALU.add).then_inc(k4_summed, 1)
                if (-1, s) in PIECE_STEPS:
                    weights_lo(PIECE_STEPS.index((-1, s)))

            def spread_group(grp):
                for e in range(E):
                    stand_at(pool, gate_applied, grp * E + (e - 1))
                    i, j = divmod(e, 4)
                    if e == 0:
                        stand_at(pool, sel_made, grp + 1)
                        row = sel[0:1, :]
                    else:
                        if e <= 4:
                            stand_at(pool, rows_in[j], grp * 16 + 16)
                        row = sel_rows[32 * i:32 * i + 1, j]
                    nc.gpsimd.partition_broadcast(sel_all[:, e % 2], row, P).then_inc(sel_spread, 1)
                    if isinstance(grp, int) and grp == 0 and (0, e - 2) in PIECE_STEPS:
                        i = PIECE_STEPS.index((0, e - 2))
                        pool.wait_ge(sel_spread, e + 1)
                        weights_lo(i)
                        pool.wait_ge(piece_lo, i + 1)

            pool.wait_ge(qk_bias_set, 2)
            spread_group(0)
            with pool.Fori(1, B * G) as grp:
                spread_group(grp)

        @block.scalar
        def _(act):
            def copy(dst, src, **kw):
                return nc.scalar.activation(dst, src, ACT.Copy, **kw)

            def wqk_split_hi():
                act.wait_ge(wqk_mean_set, 1)
                for i in range(2 * M):
                    nc.scalar.activation(wqk_hi_flat[:, i], wqk_flat[:, i], ACT.Identity,
                                         bias=minus_mean[:, i:i + 1]).then_inc(wqk_hi, 1)

            def wvl_esel_hi():
                act.wait_ge(wvl_made, 1)
                copy(wvl_h[:].rearrange("p m c -> p (m c)"), down_bank[0][:]).then_inc(wvl_hi, 1)
                act.wait_ge(constants_set, 4)
                act.wait_ge(small_in, 64)
                copy(esel_hl[:, :, 0:E], esel_raw[:])
                copy(esel_h[:, :, 0:E], esel_raw[:]).then_inc(esel_hi, 1)

            def weights_hi(i):
                act.wait_ge(piece_in[i % 2], 16 * (i // 2 + 1))
                copy(piece(i, 0), w_stage[i % 2]).then_inc(piece_hi, 1)

            def split_hi(it, s):
                sch = schedule(it)
                if s in sch["split_xT"] and has(it, 1):
                    h = sch["split_xT"][s]
                    at_least(act, xT_in, (it + 1) * (16 * G) + 16 * (h + 1))
                    at_least(act, y_projected, tile(it, GT * h + GT - 1))
                    copy(xT_h[:, h], xT_raw[:]).then_inc(xT_hi, 1)
                if s in sch["split_x"] and has(it, 1):
                    i = sch["split_x"][s]
                    at_least(act, x_in[i // 2], (it + 1) * 16 + 16)
                    at_least(act, g_added, tile(it + 1, 2 * i - (3 if first_iteration(it) else 1)))
                    copy(x_h_of(it, i), x_raw[:, 2 * i:2 * i + 2]).then_inc(x_hi, 1)

            def squares(it, b, t):
                n = tile(b, t)
                room = qk_of(it, t)
                act.wait_ge(qk_biased, n)
                at_least(act, q_transposed, pair(b - 1, t // 2))
                at_least(act, q_scale_set, b)
                nc.scalar.activation(q2[:, t], room[:, 0:C], ACT.Square,
                                     accum_out=q_sum[:, t:t + 1]).then_inc(q_squared, 1)
                at_least(act, k_summed, n - 2)
                nc.scalar.activation(k2[:, t % 2], room[:, C:2 * C], ACT.Square,
                                     accum_out=k_sum[:, t % 2:t % 2 + 1]).then_inc(k_squared, 1)
                act.wait_ge(q_squared, n)
                nc.scalar.activation(room[:, 0:C], q2[:, t], ACT.Square,
                                     accum_out=q4_sum[:, t:t + 1]).then_inc(q_fourth, 1)

            def k_normalised_hi(b, t):
                n = tile(b, t)
                act.wait_ge(k_scaled, n)
                at_least(act, g_added, n - 2)
                at_least(act, kv_projected, b)
                copy(k2_h[:, t % 2], k2[:, t % 2], scale=k_scale[:, t % 2:t % 2 + 1]).then_inc(k_hi, 1)
                at_least(act, k4_summed, n - 1)
                nc.scalar.activation(k4[:], k2[:, t % 2], ACT.Square,
                                     scale=k_scale[:, t % 2:t % 2 + 1]).then_inc(k_fourth, 1)

            def early(it, s):
                for kind, t, off in planned(it, s - 1, ("QK", "KS", "LG")):
                    if kind == "LG":
                        act.wait_ge(logits_summed, half(it + off, t))
                        nc.scalar.activation(sel[:], sel[:], ACT.Sigmoid).then_inc(sel_made, 1)
                    elif kind == "QK":
                        k_normalised_hi(it + off, t)
                        if t == T - 1:
                            act.wait_ge(q_lifted, it + off + 1)
                            nc.scalar.activation(q_root[:], q4_lifted[:], ACT.Sqrt).then_inc(q_rooted, 1)
                    else:
                        act.wait_ge(cols_copied, it + off + 1)
                        nc.scalar.activation(col_norm[:], col_sums[:, 0:M], ACT.Sqrt).then_inc(cols_rooted, 1)

            def late(it, s):
                for kind, a, off in planned(it, s - 1, ("OT",)):
                    n = out_pair(it, off, a)
                    act.wait_ge(z_shift_made, n)
                    for i in range(2 if not last_iteration(it) else 1):
                        nc.scalar.activation(z[:, a, i], z[:, a, i], ACT.Identity, bias=z_shift[:, a, i:i + 1],
                                             scale=z_rstd[:, a, i:i + 1]).then_inc(out_made, 1)
                for kind, a, off in transposed_first(
                        planned(it, s, ("QK", "GG", "KV", "QT", "Y", "XT", "LG", "OT"))):
                    b = it + off
                    if kind == "QK":
                        squares(it, b, a)
                    elif kind == "GG" and a == T - 1:
                        act.wait_ge(g_added, tile(b, a))
                        copy(gT_h[:].rearrange("p m c -> p (m c)"), g_bank[:]).then_inc(g_hi, 1)
                    elif kind == "KV":
                        for m in range(M):
                            act.wait_ge(kv_summed, b * M + m + 1)
                            act.wait_ge(cols_scaled, b + 1)
                            at_least(act, y_projected, b * T)
                            copy(kvw_h[:, m], kvw[:, m], scale=col_scale[:, m, 0:1]).then_inc(kv_hi, 1)
                    elif kind == "QT":
                        act.wait_ge(q_transposed, pair(b, a))
                        at_least(act, y_projected, tile(b, 2 * a - 3))
                        copy(qT_h[:, a % 2].rearrange("p t m n -> p (t m n)"),
                             ring_of(it, s, kind, a)[:]).then_inc(qT_hi, 1)
                    elif kind == "Y":
                        act.wait_ge(y_aggregated, tile(b, a))
                        nc.scalar.activation(y_std[:, a % 2:a % 2 + 1], y_mv[:, a % 2, 1:2], ACT.Sqrt,
                                             bias=eps_ln[:]).then_inc(y_rooted, 1)
                    elif kind == "XT":
                        g, i = divmod(a, GT)
                        act.wait_ge(x1_transposed, tile(b, a))
                        at_least(act, up_made, (b - 1) * STEPS + (g + 1) * E)
                        copy(x1T_h[:, g, :, i * P:(i + 1) * P],
                             ring_of(it, s, kind, a)[:, 0:C].rearrange("p (m n) -> p m n", m=M)
                             ).then_inc(x1T_hi, 1)
                    elif kind == "LG":
                        act.wait_ge(logits_made, half(b, a))
                        for j in range(4):
                            at_least(act, rows_in[j], b * (16 * G) + 16 * a)
                        at_least(act, sel_spread, b * STEPS + a * E - (E - 1))
                        copy(sel[:], ring_of(it, s, kind, a)[LOW:LOW + E, :]).then_inc(logits_low, 1)
                    elif kind == "OT":
                        n = out_pair(it, off, a)
                        act.wait_ge(z_aggregated, 2 * n)
                        nc.scalar.activation(z_std[:, a], z_mv[:, a, :, 1], ACT.Sqrt,
                                             bias=eps_ln[:]).then_inc(z_rooted, 1)

            def step(it, s):
                early(it, s)
                if step_exists(it, s):
                    f = step_no(it, s)
                    act.wait_ge(gate_applied, f + 1)
                    at_least(act, down_made, f - 1)
                    copy(gated_h[:, s % 2], gated[:]).then_inc(gated_hi, 1)
                late(it, s)
                if it_is(it, s, 4):
                    wqk_split_hi()
                split_hi(it, s)
                if it_is(it, s, SIGMOID_STEP):
                    nc.scalar.activation(table_ahead[:, 1:2], eps_ln[:], ACT.Sigmoid)
                if it_is(it, s, SETUP_STEPS[2]):
                    wvl_esel_hi()
                if isinstance(it, int) and (it, s) in PIECE_STEPS:
                    weights_hi(PIECE_STEPS.index((it, s)))
                if (s - LAG) % E == E - 1 and step_exists(it, s, LAG):
                    f = step_no(it, s, LAG)
                    grp = 2 * it + ((s - LAG) // E)
                    if last_iteration(it):
                        act.wait_ge(last_half_made, 1)
                    else:
                        act.wait_ge(down_made, f + 1)
                    at_least(act, o_transposed, 2 * grp)
                    if first_group(it, (s - LAG) // E):
                        act.wait_ge(piece_lo, WPIECES)
                    for m in range(M if not last_iteration(it) else 1):
                        copy(oT[:, m], down_bank[m][:]).then_inc(o_copied, 1)

            act.wait_ge(constants_set, 4)
            nc.scalar.activation(table_ahead[:, 0:1], eps_ln[:], ACT.Sqrt)
            run(act, step)

        @block.vector
        def _(dve):
            V = nc.vector

            def wqk_split_lo():
                dve.wait_ge(w_qk_in, 16)
                V.tensor_reduce(minus_mean[:], wqk_flat, AX_X, ALU.add).then_inc(wqk_summed, 1)
                dve.wait_ge(wqk_summed, 1)
                V.tensor_scalar(minus_mean[:], minus_mean[:], -1.0 / C, None, ALU.mult).then_inc(wqk_mean_set, 1)
                dve.wait_ge(wqk_mean_set, 1)
                for i in range(2 * M):
                    dve.wait_ge(wqk_hi, i + 1)
                    V.scalar_tensor_tensor(out=wqk_lo_flat[:, i], in0=wqk_flat[:, i], scalar=minus_mean[:, i:i + 1],
                                           in1=wqk_hi_flat[:, i].bitcast(F32), op0=ALU.add,
                                           op1=ALU.subtract).then_inc(wqk_lo, 1)

            def centre_qk_bias():
                dve.wait_ge(bias_in, 16)
                V.tensor_reduce(bias_mean[:], bqk_raw, AX_X, ALU.add).then_inc(bias_summed, 1)
                dve.wait_ge(bias_summed, 1)
                V.tensor_scalar(bias_mean[:], bias_mean[:], 1.0 / C, None, ALU.mult).then_inc(bias_mean_set, 1)
                dve.wait_ge(bias_mean_set, 1)
                for a in range(2):
                    V.tensor_scalar(qk_bias[:, a * C:(a + 1) * C], bqk_raw[:, a], bias_mean[:, a:a + 1],
                                    None, ALU.subtract).then_inc(qk_bias_set, 1)

            def spread_bv():
                dve.wait_ge(qk_bias_set, 2)
                dve.wait_ge(small_in, 64)
                dve.wait_ge(constants_set, 4)
                for m in range(M):
                    V.tensor_scalar(bv_wide[:, m], ones[:], bv_col[:, m:m + 1], None,
                                    ALU.mult).then_inc(bv_spread, 1)

            def wvl_esel_lo():
                dve.wait_ge(wvl_hi, 1)
                V.tensor_tensor(wvl_l[:].rearrange("p m c -> p (m c)"), down_bank[0][:],
                                wvl_h[:].bitcast(F32).rearrange("p m c -> p (m c)"),
                                ALU.subtract).then_inc(wvl_lo, 1)
                dve.wait_ge(bvl_made, 1)
                V.tensor_copy(bvl[:], down_bank[1][:, 0:C]).then_inc(bvl_copied, 1)
                dve.wait_ge(bvl_copied, 1)
                V.tensor_tensor(out_bias[:], bvl[:], bln_raw, ALU.add).then_inc(out_bias_set, 1)
                dve.wait_ge(esel_hi, 1)
                V.tensor_tensor(esel_hl[:, :, LOW:LOW + E], esel_raw[:], esel_h[:, :, 0:E].bitcast(F32),
                                ALU.subtract).then_inc(esel_lo, 1)
                dve.wait_ge(out_bias_set, 1)

            def split_lo(it, s):
                sch = schedule(it)
                if s - 1 in sch["split_xT"] and has(it, 1) and sch["split_xT"][s - 1] not in sch["gpsimd_xT"]:
                    h = sch["split_xT"][s - 1]
                    dve.wait_ge(xT_hi, half(it + 1, h))
                    V.tensor_tensor(xT_l[:, h], xT_raw[:], xT_h[:, h].bitcast(F32),
                                    ALU.subtract).then_inc(xT_lo, 1)
                if s - 1 in sch["split_x"] and has(it, 1) and sch["split_x"][s - 1] not in sch["gpsimd_x"]:
                    i = sch["split_x"][s - 1]
                    pair_x = x_raw[:, 2 * i:2 * i + 2]
                    dve.wait_ge(x_hi, pair(it + 1, i))
                    V.tensor_tensor(x_l_of(it, i), pair_x, x_h_of(it, i).bitcast(F32), ALU.subtract).then_inc(x_lo, 1)
                if s in sch["bias_x"] and has(it, 1):
                    i = sch["bias_x"][s]
                    pair_x = x_raw[:, 2 * i:2 * i + 2]
                    dve.wait_ge(x_lo, pair(it + 1, i))
                    V.tensor_tensor(pair_x, pair_x, out_bias[:].unsqueeze(1).broadcast_to((P, 2, C)),
                                    ALU.add).then_inc(x_biased, 1)

            def add_qk_bias(it, s):
                for kind, t, off in planned(it, s, ("QK",)):
                    dve.wait_ge(qk_projected, tile(it + off, t))
                    at_least(dve, q_fourth, tile(it + off, t) - (2 if first_iteration(it) else 1))
                    V.tensor_tensor(qk_of(it, t)[:], qk_bank_of(it, t)[:], qk_bias[:], ALU.add).then_inc(qk_biased, 1)

            def layer_norm(dst, src, mv, rstd):
                return V.tensor_scalar(dst, src, mv[:, 0:1], rstd, ALU.subtract, ALU.mult)

            def add_ys(it, s):
                ys = planned(it, s, ("Y",))
                for _, a, off in ys:
                    dve.wait_ge(y_projected, tile(it + off, a))
                    dve.wait_ge(x_biased, pair(it + off, a // 2))
                    at_least(dve, x1_made, tile(it + off, a) - 2)
                    V.tensor_tensor(y[:, a % 2], ring_of(it, s, "Y", a)[:, 0:C], x_raw[:, a],
                                    ALU.add).then_inc(y_added, 1)
                for _, a, off in ys:
                    dve.wait_ge(y_added, tile(it + off, a))
                    V.bn_stats(y_stats[:, a % 2], y[:, a % 2]).then_inc(y_stated, 1)
                for _, a, off in ys:
                    stand_at(dve, y_stated, tile(it + off, a))
                    V.bn_aggr(y_mv[:, a % 2], y_stats[:, a % 2]).then_inc(y_aggregated, 1)

            def finish_ys(it, s):
                ys = planned(it, s, ("Y",))
                for _, a, off in ys:
                    dve.wait_ge(y_rooted, tile(it + off, a))
                    V.reciprocal(y_rstd[:, a % 2:a % 2 + 1], y_std[:, a % 2:a % 2 + 1]).then_inc(y_inverted, 1)
                for _, a, off in ys:
                    dve.wait_ge(y_inverted, tile(it + off, a))
                    at_least(dve, x1_transposed, tile(it + off - 1, a))
                    layer_norm(x1[:, a], y[:, a % 2], y_mv[:, a % 2],
                               y_rstd[:, a % 2:a % 2 + 1]).then_inc(x1_made, 1)

            def early(it, s):
                for kind, a, off in transposed_first(
                        planned(it, s - 1, ("QK", "GG", "KS", "KV", "QT", "Y", "XT", "OT"))):
                    b = it + off
                    if kind == "Y":
                        if (kind, a, off) == planned(it, s - 1, ("Y",))[0]:
                            finish_ys(it, s - 1)
                    if kind == "QK":
                        dve.wait_ge(k_squared, tile(b, a))
                        V.tensor_scalar(k_sum_eps[:, a % 2:a % 2 + 1], k_sum[:, a % 2:a % 2 + 1], EPS_SUM,
                                        None, ALU.add).then_inc(k_eps, 1)
                        dve.wait_ge(k_eps, tile(b, a))
                        V.reciprocal(k_scale[:, a % 2:a % 2 + 1],
                                     k_sum_eps[:, a % 2:a % 2 + 1]).then_inc(k_scaled, 1)
                        if a == T - 1:
                            dve.wait_ge(q_fourth, tile(b, a))
                            V.tensor_scalar(q4_lifted[:], q4_sum[:], LIFT * LIFT, 1e-30, ALU.mult,
                                            ALU.max).then_inc(q_lifted, 1)
                            V.tensor_scalar(q_floor[:], q_sum[:], EPS_SUM, EPS_NORM * LIFT, ALU.add,
                                            ALU.mult).then_inc(q_floored, 1)
                    elif kind == "GG" and a == T - 1:
                        dve.wait_ge(g_hi, b + 1)
                        V.tensor_tensor(gT_l[:].rearrange("p m c -> p (m c)"), g_bank[:],
                                        gT_h[:].bitcast(F32).rearrange("p m c -> p (m c)"),
                                        ALU.subtract).then_inc(g_lo, 1)
                    elif kind == "KS":
                        dve.wait_ge(cols_rooted, b + 1)
                        V.reciprocal(col_scale[:], col_norm[:]).then_inc(cols_inverted, 1)
                        dve.wait_ge(cols_inverted, b + 1)
                        V.tensor_scalar(col_scale[:], col_scale[:], float(N) ** -0.5, None,
                                        ALU.mult).then_inc(cols_scaled, 1)
                    elif kind == "KV":
                        for m in range(M):
                            dve.wait_ge(kv_hi, b * M + m + 1)
                            V.scalar_tensor_tensor(out=kvw_l[:, m], in0=kvw[:, m], scalar=col_scale[:, m, 0:1],
                                                   in1=kvw_h[:, m].bitcast(F32), op0=ALU.mult,
                                                   op1=ALU.subtract).then_inc(kv_lo, 1)
                    elif kind == "QT":
                        dve.wait_ge(qT_hi, pair(b, a))
                        V.tensor_tensor(qT_l[:, a % 2].rearrange("p t m n -> p (t m n)"),
                                        ring_of(it, s - 1, kind, a)[:],
                                        qT_h[:, a % 2].bitcast(F32).rearrange("p t m n -> p (t m n)"),
                                        ALU.subtract).then_inc(qT_lo, 1)
                    elif kind == "XT":
                        g, i = divmod(a, GT)
                        dve.wait_ge(x1T_hi, tile(b, a))
                        V.tensor_tensor(x1T_l[:, g, :, i * P:(i + 1) * P],
                                        ring_of(it, s - 1, kind, a)[:, 0:C].rearrange("p (m n) -> p m n", m=M),
                                        x1T_h[:, g, :, i * P:(i + 1) * P].bitcast(F32),
                                        ALU.subtract).then_inc(x1T_lo, 1)
                    elif kind == "OT":
                        n = out_pair(it, off, a)
                        dve.wait_ge(z_rooted, n)
                        V.reciprocal(z_rstd[:, a], z_std[:, a]).then_inc(z_inverted, 1)
                        dve.wait_ge(z_inverted, n)
                        V.scalar_tensor_tensor(out=z_shift[:, a], in0=z_mv[:, a, :, 0], scalar=-1.0,
                                               in1=z_rstd[:, a], op0=ALU.mult, op1=ALU.mult
                                               ).then_inc(z_shift_made, 1)
                        if last_iteration(it):
                            layer_norm(z[:, a, 1], z[:, a, 1], z_mv[:, a, 1],
                                       z_rstd[:, a, 1:2]).then_inc(last_out_made, 1)

            def late(it, s):
                if not first_iteration(it):
                    add_qk_bias(it, s)
                for kind, a, off in planned(it, s - 1, ("QK",)):
                    n = tile(it + off, a)
                    p = a % 2
                    dve.wait_ge(k_scaled, n)
                    if a == 0:
                        at_least(dve, cols_summed, it + off)
                        V.tensor_scalar(k2_total[:], k2[:, p], k_scale[:, p:p + 1], None,
                                        ALU.mult).then_inc(k_summed, 1)
                    else:
                        dve.wait_ge(k_summed, n - 1)
                        V.scalar_tensor_tensor(out=k2_total[:], in0=k2[:, p], scalar=k_scale[:, p:p + 1],
                                               in1=k2_total[:], op0=ALU.mult, op1=ALU.add).then_inc(k_summed, 1)
                    dve.wait_ge(k_hi, n)
                    V.scalar_tensor_tensor(out=k2_l[:, p], in0=k2[:, p], scalar=k_scale[:, p:p + 1],
                                           in1=k2_h[:, p].bitcast(F32), op0=ALU.mult,
                                           op1=ALU.subtract).then_inc(k_lo, 1)
                    if a == 0:
                        dve.wait_ge(k_fourth, n)
                        V.tensor_copy(k4_total[:], k4[:]).then_inc(k4_summed, 1)
                    elif not first_iteration(it):
                        dve.wait_ge(k_fourth, n)
                        dve.wait_ge(k4_summed, n - 1)
                        V.tensor_tensor(k4_total[:], k4_total[:], k4[:], ALU.add).then_inc(k4_summed, 1)
                    if a == T - 1:
                        b = it + off
                        dve.wait_ge(q_rooted, b + 1)
                        dve.wait_ge(q_floored, b + 1)
                        V.tensor_tensor(q_root[:], q_root[:], q_floor[:], ALU.max).then_inc(q_max, 1)
                        dve.wait_ge(q_max, b + 1)
                        V.reciprocal(q_scale[:], q_root[:]).then_inc(q_scale_set, 1)
                for kind, a, off in planned(it, s, ("KS", "KV", "Y", "LG", "OT")):
                    b = it + off
                    if kind == "Y":
                        if (kind, a, off) == planned(it, s, ("Y",))[0]:
                            add_ys(it, s)
                    if kind == "KS":
                        dve.wait_ge(cols_summed, b + 1)
                        sums = ring_of(it, s, kind, a)
                        V.tensor_scalar(col_sums[:, 0:M].rearrange("p a b -> p (a b)"), sums[:, 0:2 * M],
                                        EPS_NORM ** 2, None, ALU.max)
                        V.tensor_copy(col_sums[:, M:2 * M].rearrange("p a b -> p (a b)"),
                                      sums[:, 2 * M:4 * M]).then_inc(cols_copied, 1)
                    elif kind == "KV":
                        dve.wait_ge(kv_projected, b + 1)
                        dve.wait_ge(cols_copied, b + 1)
                        for m in range(M):
                            V.scalar_tensor_tensor(out=kvw[:, m], in0=bvl[:], scalar=col_sums[:, M + m, 0:1],
                                                   in1=ring_of(it, s, kind, a)[:, m * C:(m + 1) * C],
                                                   op0=ALU.mult, op1=ALU.add).then_inc(kv_summed, 1)
                    elif kind == "LG":
                        dve.wait_ge(logits_low, half(b, a))
                        V.tensor_tensor(sel[:], ring_of(it, s, kind, a)[0:E, :], sel[:],
                                        ALU.add).then_inc(logits_summed, 1)
                    elif kind == "OT":
                        n = out_pair(it, off, a)
                        t = GT * (off % G) + 2 * a
                        dve.wait_ge(o_transposed, n)
                        at_least(dve, stored[a], it * (16 * G) + off * 16)
                        if isinstance(it, int) and it == 0:
                            dve.wait_ge(piece_lo, WPIECES)
                        V.tensor_tensor(z[:, a].rearrange("p t c -> p (t c)"), ring_of(it, s, kind, a)[:],
                                        x1[:, t:t + 2].rearrange("p t c -> p (t c)"),
                                        ALU.add).then_inc(z_added, 1)
                        dve.wait_ge(z_added, n)
                        for i in range(2):
                            V.bn_stats(z_stats[:, a, i], z[:, a, i]).then_inc(z_stated, 1)
                        for i in range(2):
                            stand_at(dve, z_stated, 2 * n - 1 + i)
                            V.bn_aggr(z_mv[:, a, i], z_stats[:, a, i]).then_inc(z_aggregated, 1)
                if s in schedule(it)["scale_q"] and has(it, 1):
                    for t in schedule(it)["scale_q"][s]:
                        dve.wait_ge(q_scale_set, it + 2)
                        V.tensor_scalar(q2[:, t], q2[:, t], q_scale[:, t:t + 1], LIFT, ALU.mult,
                                        ALU.mult).then_inc(q_scaled, 1)

            def step(it, s):
                if first_iteration(it):
                    add_qk_bias(it, s)
                early(it, s)
                if it_is(it, s, 5):
                    wqk_split_lo()
                split_lo(it, s)
                if it_is(it, s, 5):
                    centre_qk_bias()
                if it_is(it, s, SETUP_STEPS[0]):
                    spread_bv()
                if it_is(it, s, SETUP_STEPS[3]):
                    wvl_esel_lo()
                if step_exists(it, s):
                    f = step_no(it, s)
                    dve.wait_ge(up_made, f + 1)
                    dve.wait_ge(sel_spread, f + 1)
                    at_least(dve, gated_lo, f)
                    V.scalar_tensor_tensor(out=gated[:], in0=up_bank[s % 2][:], scalar=0.0,
                                           in1=sel_all[:, s % 2], op0=ALU.max,
                                           op1=ALU.mult).then_inc(gate_applied, 1)
                if last_iteration(it) and s == LAG - 1:
                    dve.wait_ge(down_made, B * STEPS)
                    at_least(dve, o_transposed, 2 * (G * B - 1))
                    V.tensor_copy(oT[:, 1], down_bank[1][:]).then_inc(o_copied, 1)
                late(it, s)
                if step_exists(it, s):
                    dve.wait_ge(gated_hi, f + 1)
                    V.tensor_tensor(gated_l[:, s % 2], gated[:],
                                    gated_h[:, s % 2].bitcast(F32), ALU.subtract).then_inc(gated_lo, 1)

            run(dve, step)

        @block.tensor
        def _(pe):
            mm = nc.tensor.matmul

            def product(dst, pairs, start, stop=True, **kw):
                n = 3 * len(pairs)
                i = 0
                for (lh, ll), (rh, rl) in pairs:
                    for lhs, rhs in ((lh, rh), (lh, rl), (ll, rh)):
                        last = mm(dst, lhs, rhs, start=start and i == 0, stop=stop and i == n - 1, **kw)
                        i += 1
                return last

            def both(hi, lo, *index):
                return hi[index], lo[index]

            def make_wvl():
                pe.wait_ge(w_v_in, 16)
                pe.wait_ge(w_ln_in, 16)
                for c in range(M):
                    for m in range(M):
                        last = mm(down_bank[0][:, c * C:(c + 1) * C], wvT_raw[:, m, c * P:(c + 1) * P],
                                  wln_raw[:, m], start=(m == 0), stop=(m == M - 1))
                last.then_inc(wvl_made, 1)
                pe.wait_ge(bv_spread, M)
                for m in range(M):
                    last = mm(down_bank[1][:, 0:C], bv_wide[:, m], wln_raw[:, m], start=(m == 0),
                              stop=(m == M - 1))
                last.then_inc(bvl_made, 1)

            pe.wait_ge(wqk_lo, 2 * M)

            ALL = slice(None)

            def layer1(it, s):
                for kind, a, off in planned(it, s, ("QK", "GG", "KS", "KV", "QT", "Y", "XT", "LG", "OT")):
                    b = it + off
                    if kind in RING_KINDS:
                        bk, read, count = ring_place(it, s, kind, a)
                        if read is not None:
                            at_least(pe, read, count)
                    if kind == "QK":
                        h, i = divmod(a, GT)
                        pe.wait_ge(xT_lo, half(b, h))
                        at_least(pe, qk_biased, tile(b, a) - (2 if first_iteration(it) else 1))
                        product(qk_bank_of(it, a)[:], [(both(xT_h, xT_l, ALL, h, m, slice(i * P, (i + 1) * P)),
                                              both(wqk_h, wqk_l, ALL, m, ALL)) for m in range(M)],
                                start=True).then_inc(qk_projected, 1)
                    elif kind == "GG":
                        pe.wait_ge(k_lo, tile(b, a))
                        pe.wait_ge(x_lo, pair(b, a // 2))
                        if a == 0:
                            at_least(pe, g_lo, b)
                        for m in range(M):
                            last = product(g_bank[:, m * C:(m + 1) * C],
                                           [(both(x_h_of(it, a // 2), x_l_of(it, a // 2), ALL, a % 2,
                                                  slice(m * P, (m + 1) * P)),
                                             both(k2_h, k2_l, ALL, a % 2, ALL))],
                                           start=(a == 0 and m == 0), stop=(a == T - 1),
                                           skip_group_check=True)
                        last.then_inc(g_added, 1)
                    elif kind == "KS":
                        pe.wait_ge(k_summed, tile(b, T - 1))
                        pe.wait_ge(k4_summed, tile(b, T - 1))
                        for i, total in enumerate((k4_total, k2_total)):
                            for m in range(M):
                                j = 2 * (i * M + m)
                                last = mm(bk[:, j:j + 2], total[:, m * P:(m + 1) * P], ones[:, 0:2],
                                          start=True, stop=True)
                        last.then_inc(cols_summed, 1)
                    elif kind == "KV":
                        pe.wait_ge(g_lo, b + 1)
                        if first_iteration(it):
                            pe.wait_ge(wvl_lo, 1)
                            pe.wait_ge(out_bias_set, 1)
                        for c in range(M):
                            last = product(bk[:, c * C:(c + 1) * C],
                                           [(both(gT_h, gT_l, ALL, m, slice(c * P, (c + 1) * P)),
                                             both(wvl_h, wvl_l, ALL, m, ALL)) for m in range(M)], start=True)
                        last.then_inc(kv_projected, 1)
                    elif kind == "QT":
                        pe.wait_ge(q_scaled, tile(b, 2 * a + 1))
                        for i in range(2):
                            for m in range(M):
                                j = (i * M + m) * P
                                last = nc.tensor.transpose(bk[:, j:j + P], q2[:, 2 * a + i, m * P:(m + 1) * P],
                                                           ident[:])
                        last.then_inc(q_transposed, 1)
                    elif kind == "Y":
                        h, i = divmod(a, GT)
                        pe.wait_ge(qT_lo, pair(b, a // 2))
                        pe.wait_ge(kv_lo, b * M + M)
                        product(bk[:, 0:C],
                                [(both(xT_h, xT_l, ALL, h, m, slice(i * P, (i + 1) * P)),
                                  both(wvl_h, wvl_l, ALL, m, ALL)) for m in range(M)] +
                                [(both(qT_h, qT_l, ALL, (a // 2) % 2, a % 2, m, ALL),
                                  both(kvw_h, kvw_l, ALL, m, ALL)) for m in range(M)],
                                start=True).then_inc(y_projected, 1)
                    elif kind == "XT":
                        pe.wait_ge(x1_made, tile(b, a))
                        for m in range(M):
                            last = nc.tensor.transpose(bk[:, m * P:(m + 1) * P], x1[:, a, m * P:(m + 1) * P],
                                                       ident[:])
                        last.then_inc(x1_transposed, 1)
                    elif kind == "LG":
                        pe.wait_ge(x1T_lo, tile(b, GT * a + GT - 1))
                        if first_iteration(it):
                            pe.wait_ge(esel_lo, 1)
                        for m in range(M):
                            mm(bk[:], esel_hl[:, m], x1T_h[:, a, m], start=(m == 0), stop=False)
                            last = mm(bk[:], esel_h[:, m], x1T_l[:, a, m], start=False, stop=(m == M - 1))
                        last.then_inc(logits_made, 1)
                    elif kind == "OT":
                        n = out_pair(it, off, a)
                        pe.wait_ge(o_copied, n - a - 1 + M)
                        for i in range(2):
                            for m in range(M):
                                j = (i * M + m) * P
                                t = 2 * a + i
                                last = nc.tensor.transpose(bk[:, j:j + P], oT[:, m, t * P:(t + 1) * P], ident[:])
                        last.then_inc(o_transposed, 1)

            def step(it, s):
                if step_exists(it, s):
                    g, e = divmod(s, E)
                    f = step_no(it, s)
                    if e == 0:
                        pe.wait_ge(x1T_lo, tile(it, GT * g + GT - 1))
                    if first_group(it, g) and e % (E // 4) == 0:
                        pe.wait_ge(piece_lo, 2 * (e // 4) + 1)
                    at_least(pe, gate_applied, f - 1)
                    product(up_bank[s % 2][:], [(both(keys_h, keys_l, ALL, e, m, ALL),
                                                 both(x1T_h, x1T_l, ALL, g, m, ALL)) for m in range(M)],
                            start=True).then_inc(up_made, 1)
                layer1(it, s)
                if it_is(it, s, SETUP_STEPS[1]):
                    make_wvl()
                if step_exists(it, s, LAG):
                    e = (s - LAG) % E
                    f = step_no(it, s, LAG)
                    grp = 2 * it + (s - LAG) // E
                    pe.wait_ge(gated_lo, f + 1)
                    if first_group(it, (s - LAG) // E) and e % (E // 4) == 0:
                        pe.wait_ge(piece_lo, 2 * (e // 4) + 2)
                    if e == 0:
                        at_least(pe, o_copied, M * grp)
                    for c in range(M):
                        r = (s - LAG) % 2
                        if c == 1 and last_iteration(it):
                            last.then_inc(last_half_made, 1)
                        last = product(down_bank[c][:], [(both(vals_h, vals_l, ALL, e, slice(c * P, (c + 1) * P)),
                                                          both(gated_h, gated_l, ALL, r, ALL))],
                                       start=(e == 0), stop=(e == E - 1))
                    last.then_inc(down_made, 1)

            run(pe, step)


def kernel(**inputs):
    import numpy as np
    import concourse.bacc as bacc
    from concourse.bass_utils import run_bass_kernel_spmd

    def given(name):
        return np.asarray(inputs["L0_" + name])

    def chunked(w):
        return w.reshape(-1, P, w.shape[-1]).transpose(1, 0, 2)

    x = given("attn_x")
    w = given("attn_Wqkv")
    b = given("attn_bqkv")
    arrays = {
        "x": x,
        "xT": x.reshape(B, P, G, GT, M, P).transpose(0, 5, 2, 4, 3, 1).reshape(B, P, G, M, GN),
        "wqk": chunked(w[:, 0:2 * C]).reshape(P, M, 2, C),
        "wvT": chunked(w[:, 2 * C:].T),
        "wln": chunked(given("attn_Wln")),
        "b_qk": b[0:2 * C].reshape(2, C),
        "b_v": b[2 * C:].reshape(M, P).T,
        "b_ln": given("attn_bln"),
        "esel": chunked(given("ffn_expert_sel").T),
        "keys": given("ffn_keys").reshape(E, M, P, H).transpose(2, 0, 1, 3).reshape(P, E * M * H),
        "values": given("ffn_values").transpose(1, 0, 2).reshape(P, E * C),
        "ident": np.eye(P, dtype=np.float32),
    }
    arrays = {name: np.ascontiguousarray(a) for name, a in arrays.items()}
    nc = bacc.Bacc("TRN2", target_bir_lowering=False, num_devices=1)
    aps = [nc.dram_tensor("in_" + name, a.shape, mybir.dt.from_np(a.dtype), kind="ExternalInput").ap()
           for name, a in arrays.items()]
    out = nc.dram_tensor("out", (B, N, C), F32, kind="ExternalOutput").ap()
    build_program(nc, *aps, out)
    r = run_bass_kernel_spmd(nc, [{"in_" + name: a for name, a in arrays.items()}], core_ids=[0])
    return r.results[0]["out"]
```
